# Optimizing a Trainium2 kernel written in Bass

```python
import numpy as np
import jax
import jax.numpy as jnp

def _softmax(x, axis=-1):
    return jax.nn.softmax(x, axis=axis)

def _gelu(x):
    return jax.nn.gelu(x, approximate=True)

def _silu(x):
    return jax.nn.silu(x)

def _sigmoid(x):
    return jax.nn.sigmoid(x)

def _layernorm(x, axis=-1, eps=1e-05):
    m = jnp.mean(x, axis=axis, keepdims=True)
    v = jnp.var(x, axis=axis, keepdims=True)
    return (x - m) / jnp.sqrt(v + eps)

def _scatter_add(tgt, idx, src, axis=0):
    return tgt.at[idx].add(src)

def _segment_sum(src, seg, n):
    return jax.ops.segment_sum(src, seg, n)
kernel_name = 'mk_recurrent_d2_jaxref_r4_12118b'

def setup_inputs(seed: int=0):
    np.random.seed(seed)
    _w = jnp.asarray

    def _L0_attn_setup():
        import jax, jax.numpy as jnp
        import numpy as np
        C = 256
        RANK = 8

        def _layernorm(x, g, b, eps=1e-05):
            mu = jnp.mean(x, axis=-1, keepdims=True)
            var = jnp.var(x, axis=-1, keepdims=True)
            return (x - mu) * jax.lax.rsqrt(var + eps) * g + b

        def _reference_tuple_inner(x, W0, A_init, B_init, log_lr, Wq, Wk, Wv, Wo, Wg, ln_g, ln_b, ls_g):
            B, T, _ = x.shape
            h = _layernorm(x, ln_g, ln_b)
            Q = jnp.einsum('btc,dc->btd', h, Wq)
            K = jnp.einsum('btc,dc->btd', h, Wk)
            V = jnp.einsum('btc,dc->btd', h, Wv)
            lr = jnp.minimum(jnp.exp(log_lr), 1.0)
            y0 = jnp.einsum('btc,cd->btd', K, W0) + jnp.einsum('btr,rd->btd', jnp.einsum('btc,cr->btr', K, A_init), B_init)
            error = y0 - V
            loss = jnp.mean(error ** 2)
            gradient = K * error
            grad_cumsum = jnp.cumsum(gradient, axis=1)
            grad_shift = jnp.concatenate([jnp.zeros((B, 1, gradient.shape[-1]), gradient.dtype), grad_cumsum[:, :-1, :]], axis=1)
            correction = Q * lr[None, None, :] * grad_shift
            pos = jnp.arange(1, T + 1, dtype=correction.dtype)
            pos_scale = (1.0 / (1.0 + 0.1 * jnp.log(pos)))[None, :, None]
            out = y0 - correction * pos_scale
            gate = jax.nn.sigmoid(jnp.einsum('btc,dc->btd', x, Wg))
            out = out * gate
            out = jnp.einsum('btc,dc->btd', out, Wo) * ls_g
            return (x + out, loss)
        key = jax.random.key(seed)
        ks = jax.random.split(key, 10)
        B, T = (4, 1024)
        x = jax.random.normal(ks[0], (B, T, C), dtype=jnp.float32)
        W0 = jnp.eye(C, dtype=jnp.float32) * 0.1
        A_init = jax.random.normal(ks[1], (C, RANK), dtype=jnp.float32) * 0.01
        B_init = jnp.zeros((RANK, C), dtype=jnp.float32)
        log_lr = jnp.full((C,), float(np.log(0.1)), dtype=jnp.float32)
        s = 1.0 / np.sqrt(C)
        Wq = jax.random.uniform(ks[2], (C, C), minval=-s, maxval=s, dtype=jnp.float32)
        Wk = jax.random.uniform(ks[3], (C, C), minval=-s, maxval=s, dtype=jnp.float32)
        Wv = jax.random.uniform(ks[4], (C, C), minval=-s, maxval=s, dtype=jnp.float32)
        Wo = jax.random.uniform(ks[5], (C, C), minval=-s, maxval=s, dtype=jnp.float32)
        Wg = jax.random.uniform(ks[6], (C, C), minval=-s, maxval=s, dtype=jnp.float32)
        ln_g = jnp.ones((C,), dtype=jnp.float32)
        ln_b = jnp.zeros((C,), dtype=jnp.float32)
        ls_g = jnp.full((C,), 0.0001, dtype=jnp.float32)
        return {'x': x, 'W0': W0, 'A_init': A_init, 'B_init': B_init, 'log_lr': log_lr, 'Wq': Wq, 'Wk': Wk, 'Wv': Wv, 'Wo': Wo, 'Wg': Wg, 'ln_g': ln_g, 'ln_b': ln_b, 'ls_g': ls_g}
    _L0_attn_in = _L0_attn_setup()

    def _L0_ffn_setup():
        import jax, jax.numpy as jnp
        import numpy as np
        B, S, D = (4, 1024, 256)
        E, F_EXP = (16, 512)
        F_C = 2.0
        F_SH = 512
        key = jax.random.key(seed)
        ks = jax.random.split(key, 8)
        s = 0.02
        return {'hidden_states': jax.random.normal(ks[0], (B, S, D), jnp.float32), 'gate_w': jax.random.normal(ks[1], (E, D), jnp.float32) * s, 'Wg': jax.random.normal(ks[2], (E, F_EXP, D), jnp.float32) * s, 'Wu': jax.random.normal(ks[3], (E, F_EXP, D), jnp.float32) * s, 'Wd': jax.random.normal(ks[4], (E, D, F_EXP), jnp.float32) * s, 'Ws_g': jax.random.normal(ks[5], (F_SH, D), jnp.float32) * s, 'Ws_u': jax.random.normal(ks[6], (F_SH, D), jnp.float32) * s, 'Ws_d': jax.random.normal(ks[7], (D, F_SH), jnp.float32) * s}
    _L0_ffn_in = _L0_ffn_setup()

    def _L1_attn_setup():
        import jax, jax.numpy as jnp
        import numpy as np
        DIM = 256
        HEADS = 16
        DIM_HEAD = 64
        INNER = HEADS * DIM_HEAD
        SCALE = DIM_HEAD ** (-0.5)

        def rotate_half(t):
            x1, x2 = jnp.split(t, 2, axis=-1)
            return jnp.concatenate((-x2, x1), axis=-1)

        def rotary_pos(n, d, dtype):
            inv_freq = 1.0 / 10000.0 ** (jnp.arange(0, d, 2, dtype=jnp.float32) / d)
            freqs = jnp.arange(n, dtype=jnp.float32)[:, None] * inv_freq[None, :]
            return jnp.concatenate((freqs, freqs), axis=-1).astype(dtype)

        def apply_rope(pos, t):
            return t * jnp.cos(pos) + rotate_half(t) * jnp.sin(pos)
        key = jax.random.key(seed)
        ks = jax.random.split(key, 5)
        x = jax.random.normal(ks[0], (2, 512, DIM), dtype=jnp.float32)
        gamma = jnp.ones((DIM,), dtype=jnp.float32)
        beta = jnp.zeros((DIM,), dtype=jnp.float32)
        Wq = jax.random.normal(ks[1], (DIM, INNER), dtype=jnp.float32) * 0.02
        Wkv = jax.random.normal(ks[2], (DIM, 2 * INNER), dtype=jnp.float32) * 0.02
        Wo = jax.random.normal(ks[3], (INNER, DIM), dtype=jnp.float32) * 0.02
        return {'x': x, 'gamma': gamma, 'beta': beta, 'Wq': Wq, 'Wkv': Wkv, 'Wo': Wo}
    _L1_attn_in = _L1_attn_setup()

    def _L1_ffn_setup():
        import jax, jax.numpy as jnp
        import numpy as np
        D, H, N, K = (256, 512, 8, 2)
        B, S = (4, 512)
        key = jax.random.key(seed)
        ks = jax.random.split(key, 4)
        x = jax.random.normal(ks[0], (B, S, D), dtype=jnp.float32)
        Wr = jax.random.normal(ks[1], (N, D), dtype=jnp.float32) / np.sqrt(D)
        br = jnp.zeros((N,), jnp.float32)
        Wl1 = jax.random.normal(ks[2], (N, D, 2 * H), dtype=jnp.float32) / np.sqrt(D)
        bl1 = jnp.zeros((N, 2 * H), jnp.float32)
        Wl2 = jax.random.normal(ks[3], (N, H, D), dtype=jnp.float32) / np.sqrt(H)
        bl2 = jnp.zeros((N, D), jnp.float32)
        biases_N = jnp.zeros((N,), jnp.float32)
        return {'x': x, 'Wr': Wr, 'br': br, 'Wl1': Wl1, 'bl1': bl1, 'Wl2': Wl2, 'bl2': bl2, 'biases_N': biases_N}
    _L1_ffn_in = _L1_ffn_setup()
    _d = {'L0_attn_x': _L0_attn_in['x'], 'L0_attn_W0': _L0_attn_in['W0'], 'L0_attn_A_init': _L0_attn_in['A_init'], 'L0_attn_B_init': _L0_attn_in['B_init'], 'L0_attn_log_lr': _L0_attn_in['log_lr'], 'L0_attn_Wq': _L0_attn_in['Wq'], 'L0_attn_Wk': _L0_attn_in['Wk'], 'L0_attn_Wv': _L0_attn_in['Wv'], 'L0_attn_Wo': _L0_attn_in['Wo'], 'L0_attn_Wg': _L0_attn_in['Wg'], 'L0_attn_ln_g': _L0_attn_in['ln_g'], 'L0_attn_ln_b': _L0_attn_in['ln_b'], 'L0_attn_ls_g': _L0_attn_in['ls_g'], 'L0_ffn_gate_w': _L0_ffn_in['gate_w'], 'L0_ffn_Wg': _L0_ffn_in['Wg'], 'L0_ffn_Wu': _L0_ffn_in['Wu'], 'L0_ffn_Wd': _L0_ffn_in['Wd'], 'L0_ffn_Ws_g': _L0_ffn_in['Ws_g'], 'L0_ffn_Ws_u': _L0_ffn_in['Ws_u'], 'L0_ffn_Ws_d': _L0_ffn_in['Ws_d'], 'L1_attn_gamma': _L1_attn_in['gamma'], 'L1_attn_beta': _L1_attn_in['beta'], 'L1_attn_Wq': _L1_attn_in['Wq'], 'L1_attn_Wkv': _L1_attn_in['Wkv'], 'L1_attn_Wo': _L1_attn_in['Wo'], 'L1_ffn_Wr': _L1_ffn_in['Wr'], 'L1_ffn_br': _L1_ffn_in['br'], 'L1_ffn_Wl1': _L1_ffn_in['Wl1'], 'L1_ffn_bl1': _L1_ffn_in['bl1'], 'L1_ffn_Wl2': _L1_ffn_in['Wl2'], 'L1_ffn_bl2': _L1_ffn_in['bl2'], 'L1_ffn_biases_N': _L1_ffn_in['biases_N']}
    _x0 = _d['L0_attn_x']
    _d['L0_attn_x'] = jax.random.normal(jax.random.fold_in(jax.random.key(seed), 1), (4, 1024, 256), dtype=_x0.dtype)
    del _x0
    return _d

def reference(L0_attn_x, L0_attn_W0, L0_attn_A_init, L0_attn_B_init, L0_attn_log_lr, L0_attn_Wq, L0_attn_Wk, L0_attn_Wv, L0_attn_Wo, L0_attn_Wg, L0_attn_ln_g, L0_attn_ln_b, L0_attn_ls_g, L0_ffn_gate_w, L0_ffn_Wg, L0_ffn_Wu, L0_ffn_Wd, L0_ffn_Ws_g, L0_ffn_Ws_u, L0_ffn_Ws_d, L1_attn_gamma, L1_attn_beta, L1_attn_Wq, L1_attn_Wkv, L1_attn_Wo, L1_ffn_Wr, L1_ffn_br, L1_ffn_Wl1, L1_ffn_bl1, L1_ffn_Wl2, L1_ffn_bl2, L1_ffn_biases_N):

    def _L0_attn_ref(x, W0, A_init, B_init, log_lr, Wq, Wk, Wv, Wo, Wg, ln_g, ln_b, ls_g):
        import jax, jax.numpy as jnp
        import numpy as np
        C = 256
        RANK = 8

        def _layernorm(x, g, b, eps=1e-05):
            mu = jnp.mean(x, axis=-1, keepdims=True)
            var = jnp.var(x, axis=-1, keepdims=True)
            return (x - mu) * jax.lax.rsqrt(var + eps) * g + b

        def _reference_tuple_inner(x, W0, A_init, B_init, log_lr, Wq, Wk, Wv, Wo, Wg, ln_g, ln_b, ls_g):
            B, T, _ = x.shape
            h = _layernorm(x, ln_g, ln_b)
            Q = jnp.einsum('btc,dc->btd', h, Wq)
            K = jnp.einsum('btc,dc->btd', h, Wk)
            V = jnp.einsum('btc,dc->btd', h, Wv)
            lr = jnp.minimum(jnp.exp(log_lr), 1.0)
            y0 = jnp.einsum('btc,cd->btd', K, W0) + jnp.einsum('btr,rd->btd', jnp.einsum('btc,cr->btr', K, A_init), B_init)
            error = y0 - V
            loss = jnp.mean(error ** 2)
            gradient = K * error
            grad_cumsum = jnp.cumsum(gradient, axis=1)
            grad_shift = jnp.concatenate([jnp.zeros((B, 1, gradient.shape[-1]), gradient.dtype), grad_cumsum[:, :-1, :]], axis=1)
            correction = Q * lr[None, None, :] * grad_shift
            pos = jnp.arange(1, T + 1, dtype=correction.dtype)
            pos_scale = (1.0 / (1.0 + 0.1 * jnp.log(pos)))[None, :, None]
            out = y0 - correction * pos_scale
            gate = jax.nn.sigmoid(jnp.einsum('btc,dc->btd', x, Wg))
            out = out * gate
            out = jnp.einsum('btc,dc->btd', out, Wo) * ls_g
            return (x + out, loss)
        return _reference_tuple_inner(x, W0, A_init, B_init, log_lr, Wq, Wk, Wv, Wo, Wg, ln_g, ln_b, ls_g)[0]

    def _L0_ffn_ref(hidden_states, gate_w, Wg, Wu, Wd, Ws_g, Ws_u, Ws_d):
        import jax, jax.numpy as jnp
        import numpy as np
        B, S, D = (4, 1024, 256)
        E, F_EXP = (16, 512)
        F_C = 2.0
        F_SH = 512
        b, s, d = hidden_states.shape
        e = gate_w.shape[0]
        cap = int(s * F_C / e)
        logits = jnp.einsum('bsd,ed->bse', hidden_states, gate_w)
        scores = jax.nn.softmax(logits, axis=-1).transpose(0, 2, 1)
        topk_w, topk_idx = jax.lax.top_k(scores, cap)
        x_tok = jnp.take_along_axis(hidden_states[:, None, :, :], topk_idx[..., None], axis=2)
        g = jnp.einsum('becd,efd->becf', x_tok, Wg)
        u = jnp.einsum('becd,efd->becf', x_tok, Wu)
        h = jax.nn.gelu(g, approximate=False) * u
        eo = jnp.einsum('becf,edf->becd', h, Wd) * topk_w[..., None]
        offs = (jnp.arange(b) * s)[:, None, None]
        flat_idx = (topk_idx + offs).reshape(-1)
        flat = jnp.zeros((b * s, d), hidden_states.dtype)
        flat = flat.at[flat_idx].add(eo.reshape(-1, d))
        out = flat.reshape(b, s, d)
        gs = jnp.einsum('bsd,fd->bsf', hidden_states, Ws_g)
        us = jnp.einsum('bsd,fd->bsf', hidden_states, Ws_u)
        shared = jnp.einsum('bsf,df->bsd', jax.nn.gelu(gs, approximate=False) * us, Ws_d)
        return out + shared

    def _L1_attn_ref(x, gamma, beta, Wq, Wkv, Wo):
        import jax, jax.numpy as jnp
        import numpy as np
        DIM = 256
        HEADS = 16
        DIM_HEAD = 64
        INNER = HEADS * DIM_HEAD
        SCALE = DIM_HEAD ** (-0.5)

        def rotate_half(t):
            x1, x2 = jnp.split(t, 2, axis=-1)
            return jnp.concatenate((-x2, x1), axis=-1)

        def rotary_pos(n, d, dtype):
            inv_freq = 1.0 / 10000.0 ** (jnp.arange(0, d, 2, dtype=jnp.float32) / d)
            freqs = jnp.arange(n, dtype=jnp.float32)[:, None] * inv_freq[None, :]
            return jnp.concatenate((freqs, freqs), axis=-1).astype(dtype)

        def apply_rope(pos, t):
            return t * jnp.cos(pos) + rotate_half(t) * jnp.sin(pos)
        b, n, _ = x.shape
        mu = jnp.mean(x, axis=-1, keepdims=True)
        var = jnp.var(x, axis=-1, keepdims=True)
        xn = (x - mu) / jnp.sqrt(var + 1e-05) * gamma + beta
        q = xn @ Wq
        kv = xn @ Wkv
        k, v = jnp.split(kv, 2, axis=-1)

        def to_heads(t):
            return t.reshape(b, n, HEADS, DIM_HEAD).transpose(0, 2, 1, 3)
        q, k, v = map(to_heads, (q, k, v))
        pos = rotary_pos(n, DIM_HEAD, x.dtype)
        q = apply_rope(pos, q)
        k = apply_rope(pos, k)
        q = q * SCALE
        sim = jnp.einsum('bhid,bhjd->bhij', q, k)
        neg = -jnp.finfo(sim.dtype).max
        causal_mask = jnp.triu(jnp.ones((n, n), dtype=bool), k=1)
        sim = jnp.where(causal_mask, neg, sim)
        attn = jax.nn.softmax(sim, axis=-1)
        out = jnp.einsum('bhij,bhjd->bhid', attn, v)
        out = out.transpose(0, 2, 1, 3).reshape(b, n, INNER)
        return out @ Wo

    def _L1_ffn_ref(x, Wr, br, Wl1, bl1, Wl2, bl2, biases_N):
        import jax, jax.numpy as jnp
        import numpy as np
        D, H, N, K = (256, 512, 8, 2)
        B, S = (4, 512)
        Bb, Ss, Dd = x.shape
        scores_BSN = jnp.einsum('bsd,nd->bsn', x, Wr) + br
        w_BSN = jax.nn.softmax(scores_BSN, axis=-1)
        _, idx_BSK = jax.lax.top_k(scores_BSN + biases_N[None, None, :], K)
        val_BSK = jnp.take_along_axis(w_BSN, idx_BSK, axis=-1)
        val_BSK = val_BSK / jnp.sum(val_BSK, axis=-1, keepdims=True)
        M = Bb * Ss
        x_MD = x.reshape(M, Dd)
        idx_MK = idx_BSK.reshape(M, K)
        val_MK = val_BSK.reshape(M, K)
        h_NM2H = jnp.einsum('md,ndh->nmh', x_MD, Wl1) + bl1[:, None, :]
        a_NMH, b_NMH = (h_NM2H[..., :H], h_NM2H[..., H:])
        y_NMD = jnp.einsum('nmh,nhd->nmd', jax.nn.silu(a_NMH) * b_NMH, Wl2) + bl2[:, None, :]
        ew_MN = jnp.zeros((M, N), x.dtype)
        ew_MN = ew_MN.at[jnp.arange(M)[:, None], idx_MK].set(val_MK)
        y_MD = jnp.einsum('mn,nmd->md', ew_MN, y_NMD)
        return y_MD.reshape(Bb, Ss, Dd)
    x = L0_attn_x
    xn = _layernorm(x, axis=-1)
    s = _L0_attn_ref(xn, L0_attn_W0, L0_attn_A_init, L0_attn_B_init, L0_attn_log_lr, L0_attn_Wq, L0_attn_Wk, L0_attn_Wv, L0_attn_Wo, L0_attn_Wg, L0_attn_ln_g, L0_attn_ln_b, L0_attn_ls_g)
    g = _silu(_L0_ffn_ref(xn, L0_ffn_gate_w, L0_ffn_Wg, L0_ffn_Wu, L0_ffn_Wd, L0_ffn_Ws_g, L0_ffn_Ws_u, L0_ffn_Ws_d))
    x = x + s * g
    xn = _layernorm(x, axis=-1)
    s = _L1_attn_ref(xn, L1_attn_gamma, L1_attn_beta, L1_attn_Wq, L1_attn_Wkv, L1_attn_Wo)
    g = _silu(_L1_ffn_ref(xn, L1_ffn_Wr, L1_ffn_br, L1_ffn_Wl1, L1_ffn_bl1, L1_ffn_Wl2, L1_ffn_bl2, L1_ffn_biases_N))
    x = x + s * g
    return x

_drawn_inputs = setup_inputs


def setup_inputs(seed=0):
    import zlib

    import numpy as np

    out = dict(_drawn_inputs(seed))
    spreads = {'L0_attn_B_init': (0.0, 0.1),
     'L0_attn_log_lr': (-2.3025851249694824, 0.2),
     'L0_attn_ln_g': (1.0, 0.2),
     'L0_attn_ln_b': (0.0, 0.1),
     'L0_attn_ls_g': (9.999999747378752e-05, 0.2),
     'L1_attn_gamma': (1.0, 0.2),
     'L1_attn_beta': (0.0, 0.1),
     'L1_ffn_br': (0.0, 0.1),
     'L1_ffn_bl1': (0.0, 0.1),
     'L1_ffn_bl2': (0.0, 0.1),
     'L1_ffn_biases_N': (0.0, 0.1)}
    factors = {}
    for name, (base, spread) in spreads.items():
        noise = np.random.default_rng([zlib.crc32(name.encode()), seed]).standard_normal(out[name].shape)
        drawn = base * np.exp(spread * noise) if base else spread * noise
        out[name] = jnp.asarray(drawn.astype(out[name].dtype))
    for name, factor in factors.items():
        out[name] = (out[name] * factor).astype(out[name].dtype)
    return out
```

```python
from contextlib import ExitStack

import numpy as np

import concourse.bass as bass
from concourse import mybir

F32 = mybir.dt.float32
F32R = mybir.dt.float32r
I32 = mybir.dt.int32
U32 = mybir.dt.uint32
ALU = mybir.AluOpType
ACT = mybir.ActivationFunctionType
AX = mybir.AxisListType.X
ds = bass.ds

P = 128
B, T, C = 4, 1024, 256
N = B * T
NT = N // P
KC = C // P
CH = 512
NCH = N // CH
TC = CH // P
RANK = 8
EPS = 1e-5

E0, F0 = 16, 512
CAP = 2 * T // E0
KF = F0 // P

HEADS, DH = 16, 64
INNER = HEADS * DH
PAIRS = HEADS // 2
TB = T // P
QKV = 3 * 2 * DH
SCALE = DH ** -0.5

E1, H1, TOP = 8, 512, 2
KH = H1 // P
SLOT_TILES = N * TOP // P + E1
SLOTS = SLOT_TILES * P


class Steps:

    def __init__(self, eng, sem, per_turn=None):
        self.eng, self.sem, self.per_turn = eng, sem, per_turn
        self.base, self.turn, self.k = 0, None, 0

    def loop(self, turn, per_turn):
        self.base, self.turn, self.per_turn, self.k = self.base + self.k, turn, per_turn, 0

    def end(self, turns):
        assert self.k == self.per_turn, (self.k, self.per_turn)
        self.base, self.turn, self.k = self.base + turns * self.per_turn, None, 0

    def done(self, ins):
        ins.then_inc(self.sem, 1)
        self.k += 1

    def wait(self):
        at = self.base + self.k
        self.eng.wait_ge(self.sem, at if self.turn is None else self.turn * self.per_turn + at)


class Scope:

    def __init__(self, nc, name, ctx):
        self.nc, self.name, self.ctx, self.held = nc, name, ctx, []
        ctx.callback(self.release)

    def sb(self, name, cols, dt=F32, rows=P):
        return self.ctx.enter_context(self.nc.sbuf_tensor(f"{self.name}_{name}", [rows, cols], dt))

    def banks(self):
        ps = self.ctx.enter_context(self.nc.psum_tensor(f"{self.name}_ps", [P, 8 * CH], F32))
        self.all_banks = ps[:, :]
        return [ps[:, i * CH:(i + 1) * CH] for i in range(8)]

    def sem(self, name):
        self.held.append(self.nc.alloc_semaphore(f"{self.name}_{name}"))
        return self.held[-1]

    def release(self):
        if self.held:
            self.nc.clear_and_free_semaphores(self.held)
            self.nc.all_engine_barrier()

    def sems(self, name, n=2):
        return [self.sem(f"{name}{i}") for i in range(n)]


def rows_of(dram, chunk):
    return dram[ds(chunk * CH, CH), :].rearrange("(t p) c -> p t c", p=P)


def tiles(ap, n=TC):
    return ap.rearrange("p (t c) -> p t c", t=n)


class Norm:

    def __init__(self, s, name):
        self.stats = s.sb(name + "_stats", NT * 6)
        self.mean, self.var, self.rstd, self.t, self.u, self.std = (s.sb(f"{name}_{x}", NT) for x in ("mean", "var", "rstd", "t", "u", "std"))
        self.var_ready, self.std_ready = s.sem(name + "_var_ready"), s.sem(name + "_std_ready")

    def spread(self, dve, st):
        q = self.stats[:, :].rearrange("p (t s) -> p t s", s=6)
        me, m2e, mo, m2o = q[:, :, 1], q[:, :, 2], q[:, :, 4], q[:, :, 5]
        st.wait()
        st.done(dve.tensor_tensor(out=self.mean[:, :], in0=me, in1=mo, op=ALU.add))
        st.done(dve.tensor_tensor(out=self.t[:, :], in0=me, in1=mo, op=ALU.subtract))
        st.done(dve.tensor_tensor(out=self.var[:, :], in0=m2e, in1=m2o, op=ALU.add))
        st.wait()
        st.done(dve.tensor_scalar(self.mean[:, :], self.mean[:, :], 0.5, None, ALU.mult))
        st.done(dve.scalar_tensor_tensor(out=self.u[:, :], in0=self.t[:, :], scalar=0.25, in1=self.t[:, :], op0=ALU.mult, op1=ALU.mult))
        st.done(dve.tensor_scalar(self.var[:, :], self.var[:, :], 1.0 / C, EPS, ALU.mult, ALU.add))
        st.wait()
        dve.tensor_tensor(out=self.var[:, :], in0=self.var[:, :], in1=self.u[:, :], op=ALU.add).then_inc(self.var_ready, 1)

    def root(self, act):
        act.wait_ge(self.var_ready, 1)
        act.activation(self.std[:, :], self.var[:, :], ACT.Sqrt).then_inc(self.std_ready, 1)

    def invert(self, dve, st):
        dve.wait_ge(self.std_ready, 1)
        st.done(dve.reciprocal(self.rstd[:, :], self.std[:, :]))
        st.wait()
        st.done(dve.tensor_tensor(out=self.t[:, :], in0=self.var[:, :], in1=self.rstd[:, :], op=ALU.mult))
        st.wait()
        st.done(dve.tensor_tensor(out=self.t[:, :], in0=self.t[:, :], in1=self.rstd[:, :], op=ALU.mult))
        st.wait()
        st.done(dve.tensor_scalar(self.t[:, :], self.t[:, :], -0.5, 1.5, ALU.mult, ALU.add))
        st.wait()
        st.done(dve.tensor_tensor(out=self.rstd[:, :], in0=self.rstd[:, :], in1=self.t[:, :], op=ALU.mult))
        st.wait()


def normalize(nc, name, d, first):
    with ExitStack() as ctx:
        s = Scope(nc, name, ctx)
        n_exp = E0 if first else E1
        x = s.sb("x", NT * C)
        stage = [s.sb(f"stage{u}", TC * C) for u in range(2)]
        ident = s.sb("ident", P)
        gate_w = s.sb("gate_w", KC * n_exp)
        gain, off = s.sb("gain", KC), s.sb("off", KC)
        nx, nh = Norm(s, "nx"), Norm(s, "nh")
        logT = s.sb("logT", N, rows=n_exp)
        xT = d.xnT if first else None
        turned = [s.sb(f"turned{u}", KC * CH) for u in range(2)]
        if not first:
            sg = [s.sb(f"s{u}", TC * C) for u in range(2)]
            zg = [s.sb(f"z{u}", TC * C) for u in range(2)]
            th = [s.sb(f"th{u}", TC * C) for u in range(2)]
        ps = s.banks()
        consts = s.sem("consts")
        x_in = s.sems("x_in", 8)
        dve_steps = s.sem("dve_steps")
        x_added = s.sem("x_added")
        loaded, squashed, gated = s.sems("loaded"), s.sems("squashed"), s.sems("gated")
        stage_ready = s.sems("stage_ready")
        turned_ps = s.sems("turned_ps")
        turned_sb = s.sems("turned_sb")
        stored = s.sems("stored")
        log_ps, log_sb = s.sems("log_ps"), s.sems("log_sb")
        x_stored = s.sem("x_stored")
        logs_stored = s.sem("logs_stored")
        H = NCH // 2

        with nc.Block() as block:
            @block.sync
            def _(sp):
                sp.dma_start(ident[:, :], d.ident).then_inc(consts, 16)
                sp.dma_start(gate_w[:, :], d.gate_w[name]).then_inc(consts, 16)
                sp.dma_start(gain[:, :], d.gain[name]).then_inc(consts, 16)
                sp.dma_start(off[:, :], d.off[name]).then_inc(consts, 16)
                for g in range(NCH):
                    sp.dma_start(tiles(x[:, g * TC * C:(g + 1) * TC * C]), rows_of(d.x, g)).then_inc(x_in[g], 16)
                if not first:
                    with sp.Fori(0, H) as i:
                        for u in range(2):
                            sp.wait_ge(gated[u], i)
                            sp.dma_start(tiles(sg[u][:, :]), rows_of(d.s, i * 2 + u)).then_inc(loaded[u], 16)
                            sp.dma_start(tiles(zg[u][:, :]), rows_of(d.z, i * 2 + u)).then_inc(loaded[u], 16)
                    sp.wait_ge(x_added, NCH)
                    sp.dma_start(d.x2.rearrange("(t p) c -> p t c", p=P), tiles(x[:, :], NT)).then_inc(x_stored, 16)
                with sp.Fori(0, H) as i:
                    for u in range(2):
                        sp.wait_ge(stage_ready[u], i + 1)
                        sp.dma_start(rows_of(d.xn[name], i * 2 + u), tiles(stage[u][:, :])).then_inc(stored[u], 16)
                if not first:
                    with sp.Fori(0, H) as i:
                        for u in range(2):
                            sp.wait_ge(turned_sb[u], KC * H + KC * (i + 1))
                            for c in range(KC):
                                sp.dma_start(d.hT1[c * P:(c + 1) * P, ds(i * T + u * CH, CH)],
                                             turned[u][:, c * CH:(c + 1) * CH]).then_inc(stored[u], 16)
                for u in range(2):
                    sp.wait_ge(log_sb[u], H)
                sp.dma_start(d.logT[name], logT[:, :]).then_inc(logs_stored, 16)
                sp.wait_ge(logs_stored, 16)
                for u in range(2):
                    sp.wait_ge(stored[u], 16 * H * (1 if first else 1 + KC))
                if not first:
                    sp.wait_ge(x_stored, 16)

            @block.vector
            def _(dve):
                st = Steps(dve, dve_steps)
                if first:
                    for g in range(NCH):
                        dve.wait_ge(x_in[g], 16)
                        for t in range(g * TC, (g + 1) * TC):
                            st.done(dve.bn_stats(nx.stats[:, t * 6:t * 6 + 6], x[:, t * C:(t + 1) * C]))
                else:
                    for g in range(NCH):
                        dve.wait_ge(x_in[g], 16)
                    with dve.Fori(0, H) as i:
                        st.loop(i, 2 * (2 + TC))
                        for u in range(2):
                            dve.wait_ge(squashed[u], i + 1)
                            st.done(dve.scalar_tensor_tensor(out=zg[u][:, :], in0=th[u][:, :], scalar=1.0, in1=zg[u][:, :], op0=ALU.add, op1=ALU.mult))
                            st.wait()
                            st.done(dve.tensor_tensor(out=sg[u][:, :], in0=zg[u][:, :], in1=sg[u][:, :], op=ALU.mult))
                            st.wait()
                            xg = x[:, ds(i * (2 * TC * C) + u * TC * C, TC * C)]
                            dve.scalar_tensor_tensor(out=xg, in0=sg[u][:, :], scalar=0.5, in1=xg, op0=ALU.mult, op1=ALU.add).then_inc(x_added, 1)
                            dve.wait_ge(x_added, i * 2 + u + 1)
                            for t in range(TC):
                                ins = dve.bn_stats(nx.stats[:, ds(i * (2 * TC * 6) + (u * TC + t) * 6, 6)],
                                                   x[:, ds(i * (2 * TC * C) + (u * TC + t) * C, C)])
                                st.done(ins)
                            dve.nop().then_inc(gated[u], 1)
                    st.end(H)
                nx.spread(dve, st)
                nx.invert(dve, st)
                with dve.Fori(0, H) as i:
                    st.loop(i, 2 * 2 * TC)
                    for u in range(2):
                        dve.wait_ge(turned_ps[u], KC * i)
                        dve.wait_ge(stored[u], 16 * i)
                        for t in range(TC):
                            at = i * (2 * TC) + (u * TC + t)
                            ins = dve.tensor_scalar(stage[u][:, t * C:(t + 1) * C], x[:, ds(at * C, C)],
                                                    nx.mean[:, ds(at, 1)], nx.rstd[:, ds(at, 1)], ALU.subtract, ALU.mult)
                            st.done(ins)
                        st.wait()
                        dve.nop().then_inc(stage_ready[u], 1)
                        for t in range(TC):
                            at = i * (2 * TC) + (u * TC + t)
                            st.done(dve.bn_stats(nh.stats[:, ds(at * 6, 6)], stage[u][:, t * C:(t + 1) * C]))
                st.end(H)
                nh.spread(dve, st)
                nh.invert(dve, st)
                st.done(dve.reciprocal(nx.t[:, :], nx.rstd[:, :]))
                st.wait()
                st.done(dve.tensor_tensor(out=nx.t[:, :], in0=nx.t[:, :], in1=nh.mean[:, :], op=ALU.mult))
                st.done(dve.tensor_tensor(out=nh.rstd[:, :], in0=nx.rstd[:, :], in1=nh.rstd[:, :], op=ALU.mult))
                st.wait()
                st.done(dve.tensor_tensor(out=nh.mean[:, :], in0=nx.t[:, :], in1=nx.mean[:, :], op=ALU.add))
                st.wait()
                with dve.Fori(0, H) as i:
                    st.loop(i, 2 * TC)
                    for u in range(2):
                        dve.wait_ge(turned_ps[u], KC * H + KC * i)
                        dve.wait_ge(stored[u], 16 * H)
                        for t in range(TC):
                            at = i * (2 * TC) + (u * TC + t)
                            st.done(dve.tensor_scalar(stage[u][:, t * C:(t + 1) * C], x[:, ds(at * C, C)],
                                                      nh.mean[:, ds(at, 1)], nh.rstd[:, ds(at, 1)], ALU.subtract, ALU.mult))
                        st.wait()
                        dve.nop().then_inc(stage_ready[u], 1)
                st.end(H)

            @block.tensor
            def _(pe):
                pe.wait_ge(consts, 64)

                def turn(i, u, sweep):
                    pe.wait_ge(stage_ready[u], i + 1 + sweep * H)
                    for c in range(KC):
                        pe.wait_ge(turned_sb[u], KC * (i + sweep * H))
                        for t in range(TC):
                            last = pe.transpose(ps[2 * u + c][:, t * P:(t + 1) * P],
                                                stage[u][:, t * C + c * P:t * C + (c + 1) * P], ident[:, :])
                        last.then_inc(turned_ps[u], 1)

                with pe.Fori(0, H) as i:
                    for u in range(2):
                        turn(i, u, 0)
                        pe.wait_ge(turned_sb[u], KC * (i + 1))
                        pe.wait_ge(log_sb[u], i)
                        for c in range(KC):
                            src = turned[u][:, c * CH:(c + 1) * CH]
                            last = pe.matmul(ps[4 + u][0:n_exp, :], gate_w[:, c * n_exp:(c + 1) * n_exp], src,
                                             start=c == 0, stop=c == KC - 1)
                        last.then_inc(log_ps[u], 1)
                with pe.Fori(0, H) as i:
                    for u in range(2):
                        turn(i, u, 1)

            @block.scalar
            def _(act):
                if not first:
                    with act.Fori(0, H) as i:
                        for u in range(2):
                            act.wait_ge(loaded[u], 32 * (i + 1))
                            act.wait_ge(gated[u], i)
                            act.activation(th[u][:, :], zg[u][:, :], ACT.Tanh, scale=0.5).then_inc(squashed[u], 1)
                nx.root(act)
                with act.Fori(0, H) as i:
                    for u in range(2):
                        act.wait_ge(log_ps[u], i)
                        for c in range(KC):
                            act.wait_ge(turned_ps[u], KC * i + c + 1)
                            act.activation(turned[u][:, c * CH:(c + 1) * CH], ps[2 * u + c], ACT.Copy).then_inc(turned_sb[u], 1)
                            if first:
                                act.activation(xT[:, ds(i * (2 * CH) + c * N + u * CH, CH)], ps[2 * u + c], ACT.Copy)
                        act.wait_ge(log_ps[u], i + 1)
                        act.activation(logT[:, ds(i * (2 * CH) + u * CH, CH)], ps[4 + u][0:n_exp, :], ACT.Copy).then_inc(log_sb[u], 1)
                nh.root(act)
                act.wait_ge(consts, 64)
                with act.Fori(0, H) as i:
                    for u in range(2):
                        if not first:
                            act.wait_ge(stored[u], 16 * H + 16 * KC * i)
                        for c in range(KC):
                            act.wait_ge(turned_ps[u], KC * H + KC * i + c + 1)
                            dst = d.hT[:, ds(i * (2 * CH) + c * N + u * CH, CH)] if first else turned[u][:, c * CH:(c + 1) * CH]
                            act.activation(dst, ps[2 * u + c], ACT.Identity, scale=gain[:, c:c + 1], bias=off[:, c:c + 1]).then_inc(turned_sb[u], 1)


def bcast(ap, n):
    return ap.unsqueeze(2).to_broadcast([ap.shape[0], ap.shape[1], n])


def first_layer(nc, d):
    with ExitStack() as ctx:
        s = Scope(nc, "l0", ctx)
        wq, wk, wv, wg, w0 = (s.sb(x, KC * C) for x in ("wq", "wk", "wv", "wg", "w0"))
        wo = s.sb("wo", KC * C)
        lr_at = s.sb("lr", KC)
        ls = s.sb("ls", C)
        a_t, b_t = s.sb("a_t", C, rows=RANK), s.sb("b_t", C, rows=RANK)
        pos = s.sb("pos", T)
        ones = s.sb("ones", CH)
        sg, su, sd = s.sb("sg", KC * F0), s.sb("su", KC * F0), s.sb("sd", KF * C)
        ident = s.sb("ident", P)
        row0 = s.sb("row0", 1, rows=B * E0)
        logT = s.sb("logT", N, rows=E0)
        probs, top1 = s.sb("probs", NT * E0), s.sb("top1", NT)
        work = s.sb("work", T, rows=B * E0)
        best, best_at = s.sb("best", 8, rows=B * E0), s.sb("best_at", 8, U32, rows=B * E0)
        picks_w, picks_at = s.sb("picks_w", CAP, rows=B * E0), s.sb("picks_at", CAP, rows=B * E0)
        k_sb, y_sb, t_sb, e_sb, th = ([s.sb(f"{n}{c}", CH) for c in range(KC)] for n in ("k", "y", "t", "e", "th"))
        cs = [[s.sb(f"cs{u}{c}", CH + 1) for c in range(KC)] for u in range(2)]
        o_sb = [s.sb(f"o{c}", CH) for c in range(KC)]
        gel = [s.sb(f"gel{j}", CH) for j in range(2)]
        hid = [s.sb(f"hid{f}", CH) for f in range(KF)]
        xr = [s.sb(f"xr{u}", TC * C) for u in range(2)]
        z_st = [s.sb(f"z{u}", TC * C) for u in range(2)]
        ps = s.banks()

        consts, router_in = s.sem("consts"), s.sem("router_in")
        prep, prep_ps = s.sem("prep"), s.sem("prep_ps")
        lr_exp = s.sem("lr_exp")
        rt_ps, rt_dve, rt_act, rows_ps, rows_sb = (s.sem(x) for x in ("rt_ps", "rt_dve", "rt_act", "rows_ps", "rows_sb"))
        picked, picks_ps = s.sem("picked"), s.sem("picks_ps")
        k_ps, v_ps, y_ps, q_ps, g_ps, o_ps, ffn_ps, dn_ps = (s.sem(x) for x in ("k_ps", "v_ps", "y_ps", "q_ps", "g_ps", "o_ps", "ffn_ps", "dn_ps"))
        k_done, y_done, th_done, gel_done, dn_done = (s.sem(x) for x in ("k_done", "y_done", "th_done", "gel_done", "dn_done"))
        v_read, q_read, o_done, hid_done, s_done = (s.sem(x) for x in ("v_read", "q_read", "o_done", "hid_done", "s_done"))
        dve_steps = s.sem("dve_steps")
        xr_in, s_made, s_out, z_out = s.sems("xr_in"), s.sems("s_made"), s.sems("s_out"), s.sems("z_out")
        z_made = s.sems("z_made")
        HB = NCH // 2
        N_CONST = 15

        with nc.Block() as block:
            @block.sync
            def _(sp):
                sp.dma_start(logT[:, :], d.logT["n0"]).then_inc(router_in, 16)
                sp.dma_start(ident[:, :], d.ident).then_inc(router_in, 16)
                for dst, src in ((a_t, d.w["A"]), (b_t, d.w["B"]), (w0, d.w["W0"]), (wo, d.w["Wo"]), (ls, d.w["ls"]),
                                 (lr_at, d.w["lr"]), (wk, d.w["Wk"]), (wv, d.w["Wv"]), (sg, d.w["Ws_g"]), (su, d.w["Ws_u"]),
                                 (sd, d.w["Ws_d"]), (wq, d.w["Wq"]), (wg, d.w["Wg"]), (pos, d.pos), (row0, d.row0)):
                    sp.dma_start(dst[:, :], src).then_inc(consts, 16)
                with sp.Fori(0, HB) as i:
                    for u in range(2):
                        sp.wait_ge(s_out[u], 16 * i)
                        sp.dma_start(tiles(xr[u][:, :]), rows_of(d.xn["n0"], i * 2 + u)).then_inc(xr_in[u], 16)
                    for u in range(2):
                        sp.wait_ge(z_made[u], i + 1)
                        sp.dma_start(rows_of(d.z, i * 2 + u), tiles(z_st[u][:, :])).then_inc(z_out[u], 16)
                        sp.wait_ge(s_made[u], i + 1)
                        sp.dma_start(rows_of(d.s, i * 2 + u), tiles(xr[u][:, :])).then_inc(s_out[u], 16)
                for u in range(2):
                    sp.wait_ge(z_out[u], 16 * HB)
                    sp.wait_ge(s_out[u], 16 * HB)

            @block.tensor
            def _(pe):
                pe.wait_ge(router_in, 32)
                for t in range(NT):
                    b, j = t // TB, t % TB
                    at = (j * B + b) * E0
                    last = pe.transpose(ps[4][:, at:at + E0], logT[:, t * P:(t + 1) * P], ident[0:E0, 0:E0])
                last.then_inc(rt_ps, 1)
                pe.wait_ge(consts, 16 * N_CONST)
                for c in range(KC):
                    last = pe.matmul(ps[5][:, c * C:(c + 1) * C], a_t[:, c * P:(c + 1) * P], b_t[:, :], start=True, stop=True)
                last.then_inc(prep_ps, 1)
                pe.wait_ge(rt_dve, 1)
                for j in range(TB):
                    bank = 6 + j // 4
                    last = pe.transpose(ps[bank][0:B * E0, (j % 4) * P:(j % 4 + 1) * P], probs[:, j * B * E0:(j + 1) * B * E0], ident[:, :])
                last.then_inc(rows_ps, 1)
                pe.wait_ge(prep, 2)
                pe.wait_ge(rows_sb, 2)

                def project(bank, w, c, rhs, signal):
                    for k in range(KC):
                        last = pe.matmul(bank, w[:, k * C + c * P:k * C + (c + 1) * P], rhs(k), start=k == 0, stop=k == KC - 1)
                    last.then_inc(signal, 1)

                with pe.Fori(0, HB) as i:
                    for u in range(2):
                        g = i * 2 + u

                        def h(k):
                            return d.hT[:, ds(i * T + k * N + u * CH, CH)]

                        def xn(k):
                            return d.xnT[:, ds(i * T + k * N + u * CH, CH)]

                        def up(f):
                            pair = ps[4 + 2 * (f % 2):6 + 2 * (f % 2)]
                            for w, bank in zip((sg, su), pair):
                                for k in range(KC):
                                    last = pe.matmul(bank, w[:, k * F0 + f * P:k * F0 + (f + 1) * P], xn(k), start=k == 0, stop=k == KC - 1)
                            last.then_inc(ffn_ps, 1)

                        pe.wait_ge(th_done, 2 * g)
                        for c in range(KC):
                            project(ps[c], wk, c, h, k_ps)
                        pe.wait_ge(s_done, 2 * g)
                        for c in range(KC):
                            project(ps[2 + c], wv, c, h, v_ps)
                        pe.wait_ge(dn_done, 2 * g)
                        up(0)
                        pe.wait_ge(hid_done, 4 * g)
                        up(1)
                        pe.wait_ge(k_done, 2 * g + 2)
                        for c in range(KC):
                            project(ps[c], w0, c, lambda k: k_sb[k][:, :], y_ps)
                        pe.wait_ge(hid_done, 4 * g + 1)
                        up(2)
                        for c in range(KC):
                            pe.wait_ge(v_read, 2 * g + c + 1)
                            project(ps[2 + c], wq, c, h, q_ps)
                        for c in range(KC):
                            pe.wait_ge(y_done, 2 * g + c + 1)
                            project(ps[c], wg, c, xn, g_ps)
                        pe.wait_ge(hid_done, 4 * g + 2)
                        up(3)
                        pe.wait_ge(hid_done, 4 * g + 4)
                        for t in range(TC):
                            for f in range(KF):
                                last = pe.matmul(ps[4 + t // 2][:, (t % 2) * C:(t % 2 + 1) * C], hid[f][:, t * P:(t + 1) * P],
                                                 sd[:, f * C:(f + 1) * C], start=f == 0, stop=f == KF - 1)
                            if t % 2:
                                last.then_inc(dn_ps, 1)
                        pe.wait_ge(q_read, 2 * g + 2)
                        pe.wait_ge(o_done, 2 * g + 2)
                        for t in range(TC):
                            for k in range(KC):
                                last = pe.matmul(ps[2 + t // 2][:, (t % 2) * C:(t % 2 + 1) * C], o_sb[k][:, t * P:(t + 1) * P],
                                                 wo[:, k * C:(k + 1) * C], start=k == 0, stop=k == KC - 1)
                            if t % 2:
                                last.then_inc(o_ps, 1)
                pe.wait_ge(picked, 1)
                pe.wait_ge(dn_done, 2 * NCH)
                pe.transpose(ps[4][:, 0:B * E0], picks_at[:, :], ident[0:B * E0, 0:B * E0])
                pe.transpose(ps[4][:, B * E0:2 * B * E0], picks_w[:, :], ident[0:B * E0, 0:B * E0]).then_inc(picks_ps, 1)

            @block.scalar
            def _(act):
                act.wait_ge(rt_act, 1)
                act.activation(probs[:, :], probs[:, :], ACT.Exp).then_inc(rt_act, 1)
                act.wait_ge(consts, 16 * N_CONST)
                act.activation(lr_at[:, :], lr_at[:, :], ACT.Exp).then_inc(lr_exp, 1)
                act.wait_ge(rows_ps, 1)
                for j in range(2):
                    act.activation(work[:, j * CH:(j + 1) * CH], ps[6 + j][0:B * E0, :], ACT.Copy).then_inc(rows_sb, 1)
                with act.Fori(0, HB) as i:
                    for u in range(2):
                        g = i * 2 + u

                        def gelu(f):
                            act.wait_ge(ffn_ps, 4 * g + f + 1)
                            act.activation(gel[f % 2][:, :], ps[4 + 2 * (f % 2)], ACT.Gelu).then_inc(gel_done, 1)

                        for c in range(KC):
                            act.wait_ge(k_ps, 2 * g + c + 1)
                            act.activation(k_sb[c][:, :], ps[c], ACT.Copy).then_inc(k_done, 1)
                        gelu(0)
                        gelu(1)
                        for c in range(KC):
                            act.wait_ge(y_ps, 2 * g + c + 1)
                            act.activation(y_sb[c][:, :], ps[c], ACT.Copy).then_inc(y_done, 1)
                        gelu(2)
                        for c in range(KC):
                            act.wait_ge(g_ps, 2 * g + c + 1)
                            act.activation(th[c][:, :], ps[c], ACT.Tanh, scale=0.5).then_inc(th_done, 1)
                        gelu(3)
                        act.wait_ge(z_out[u], 16 * i)
                        for j in range(2):
                            act.wait_ge(dn_ps, 2 * g + j + 1)
                            act.activation(z_st[u][:, j * 2 * C:(j + 1) * 2 * C], ps[4 + j], ACT.Copy).then_inc(dn_done, 1)
                        act.wait_ge(dn_done, 2 * g + 2)
                        act.nop().then_inc(z_made[u], 1)

            @block.vector
            def _(dve):
                st = Steps(dve, dve_steps)
                p3 = probs[:, :].rearrange("p (t e) -> p t e", e=E0)
                dve.wait_ge(rt_ps, 1)
                st.done(dve.tensor_reduce(out=top1[:, :], in_=ps[4].rearrange("p (t e) -> p t e", e=E0), axis=AX, op=ALU.max))
                st.wait()
                dve.tensor_tensor(out=p3, in0=ps[4].rearrange("p (t e) -> p t e", e=E0), in1=bcast(top1[:, :], E0), op=ALU.subtract).then_inc(rt_act, 1)
                dve.wait_ge(rt_act, 2)
                st.done(dve.tensor_reduce(out=top1[:, :], in_=p3, axis=AX, op=ALU.add))
                st.wait()
                st.done(dve.reciprocal(top1[:, :], top1[:, :]))
                st.wait()
                dve.tensor_tensor(out=p3, in0=p3, in1=bcast(top1[:, :], E0), op=ALU.mult).then_inc(rt_dve, 1)
                dve.wait_ge(prep_ps, 1)
                dve.tensor_tensor(out=w0[:, :], in0=ps[5], in1=w0[:, :], op=ALU.add).then_inc(prep, 1)
                for k in range(KC):
                    ins = dve.scalar_tensor_tensor(out=wo[:, k * C:(k + 1) * C], in0=wo[:, k * C:(k + 1) * C], scalar=0.5,
                                                   in1=ls[:, :], op0=ALU.mult, op1=ALU.mult)
                ins.then_inc(prep, 1)
                dve.wait_ge(lr_exp, 1)
                st.done(dve.tensor_scalar(lr_at[:, :], lr_at[:, :], 1.0, None, ALU.min))
                st.done(dve.memset(ones[:, :], 1.0))
                for c in range(KC):
                    st.done(dve.memset(cs[0][c][:, 0:1], 0.0))
                st.wait()
                dve.wait_ge(rows_sb, 2)
                with dve.Fori(0, HB) as i:
                    st.loop(i, 2 * (2 * 3 + 4 * KC) + KC)
                    for u in range(2):
                        g = i * 2 + u

                        def hidden(f):
                            dve.wait_ge(gel_done, 4 * g + f + 1)
                            dve.tensor_tensor(out=hid[f][:, :], in0=gel[f % 2][:, :], in1=ps[5 + 2 * (f % 2)], op=ALU.mult).then_inc(hid_done, 1)

                        def pick(r):
                            st.done(dve.max(best[:, :], work[:, :]))
                            st.wait()
                            at = i * 32 + (u * 2 + r) * 8
                            dve.tensor_copy(picks_w[:, ds(at, 8)], best[:, :])
                            dve.max_index(best_at[:, :], best[:, :], work[:, :])
                            st.done(dve.match_replace(work[:, :], best[:, :], work[:, :], -1.0))
                            st.wait()
                            st.done(dve.tensor_copy(picks_at[:, ds(at, 8)], best_at[:, :]))
                            st.wait()

                        hidden(0)
                        pick(0)
                        hidden(1)
                        pick(1)
                        for c in range(KC):
                            dve.wait_ge(y_done, 2 * g + c + 1)
                            dve.wait_ge(v_ps, 2 * g + c + 1)
                            st_ins = dve.tensor_tensor(out=e_sb[c][:, :], in0=y_sb[c][:, :], in1=ps[2 + c], op=ALU.subtract)
                            st_ins.then_inc(v_read, 1)
                        hidden(2)
                        dve.wait_ge(v_read, 2 * g + 2)
                        for c in range(KC):
                            st.done(dve.tensor_tensor(out=e_sb[c][:, :], in0=e_sb[c][:, :], in1=k_sb[c][:, :], op=ALU.mult))
                            if u == 1:
                                st.done(dve.tensor_copy(cs[1][c][:, 0:1], cs[0][c][:, CH:CH + 1]))
                        st.wait()
                        for c in range(KC):
                            st.done(dve.tensor_tensor_scan(out=cs[u][c][:, 1:CH + 1], data0=ones[:, :], data1=e_sb[c][:, :],
                                                           initial=cs[u][c][:, 0:1], op0=ALU.mult, op1=ALU.add))
                        for c in range(KC):
                            dve.wait_ge(q_ps, 2 * g + c + 1)
                            ins = dve.scalar_tensor_tensor(out=t_sb[c][:, :], in0=ps[2 + c], scalar=lr_at[:, c:c + 1],
                                                           in1=pos[:, u * CH:(u + 1) * CH], op0=ALU.mult, op1=ALU.mult)
                            ins.then_inc(q_read, 1)
                        dve.wait_ge(q_read, 2 * g + 2)
                        st.wait()
                        for c in range(KC):
                            st.done(dve.tensor_tensor(out=t_sb[c][:, :], in0=t_sb[c][:, :], in1=cs[u][c][:, 0:CH], op=ALU.mult))
                        hidden(3)
                        st.wait()
                        for c in range(KC):
                            st.done(dve.tensor_tensor(out=t_sb[c][:, :], in0=y_sb[c][:, :], in1=t_sb[c][:, :], op=ALU.subtract))
                        st.wait()
                        for c in range(KC):
                            dve.wait_ge(th_done, 2 * g + c + 1)
                            dve.scalar_tensor_tensor(out=o_sb[c][:, :], in0=th[c][:, :], scalar=1.0, in1=t_sb[c][:, :],
                                                     op0=ALU.add, op1=ALU.mult).then_inc(o_done, 1)
                        dve.wait_ge(xr_in[u], 16 * (i + 1))
                        for j in range(2):
                            dve.wait_ge(o_ps, 2 * g + j + 1)
                            half = xr[u][:, j * 2 * C:(j + 1) * 2 * C]
                            dve.tensor_tensor(out=half, in0=half, in1=ps[2 + j], op=ALU.add).then_inc(s_done, 1)
                        dve.wait_ge(s_done, 2 * g + 2)
                        dve.nop().then_inc(s_made[u], 1)
                st.end(HB)
                st.done(dve.tensor_scalar(picks_at[:, :], picks_at[:, :], row0[:, 0:1], None, ALU.add))
                st.wait()
                dve.nop().then_inc(picked, 1)
                dve.wait_ge(picks_ps, 1)
                dve.tensor_copy(d.slot_row[:, :], ps[4][:, 0:B * E0])
                st.done(dve.tensor_copy(d.slot_w[:, :], ps[4][:, B * E0:2 * B * E0]))
                st.wait()


def experts(nc, d):
    with ExitStack() as ctx:
        s = Scope(nc, "ex", ctx)
        wg, wu, wd = ([s.sb(f"{n}{u}", w) for u in range(2)] for n, w in (("wg", KC * F0), ("wu", KC * F0), ("wd", KF * C)))
        ident = s.sb("ident", P)
        rows = [s.sb(f"rows{u}", B, I32) for u in range(2)]
        xg = [s.sb(f"xg{u}", B * C) for u in range(2)]
        xT = [[s.sb(f"xT{u}{c}", B * CAP) for c in range(KC)] for u in range(2)]
        gel = [s.sb(f"gel{j}", B * CAP) for j in range(2)]
        hid = [s.sb(f"hid{f}", B * CAP) for f in range(KF)]
        eo = [s.sb(f"eo{u}", B * C) for u in range(2)]
        ps = s.banks()
        consts, picked, go = s.sem("consts"), s.sem("picked"), s.sem("go")
        w_in, gathered, scattered = s.sems("w_in"), s.sems("gathered"), s.sems("scattered")
        t_ps, xt_done, ffn_ps, gel_done, hid_done, dn_ps, eo_done = (s.sem(x) for x in ("t_ps", "xt_done", "ffn_ps", "gel_done", "hid_done", "dn_ps", "eo_done"))
        HE = E0 // 2

        with nc.Block() as block:
            @block.sync
            def _(sp):
                sp.dma_start(ident[:, :], d.ident).then_inc(consts, 16)

                def load(e, u):
                    sp.dma_start(wg[u][:, :], d.w["eg"][ds(e * P, P), :]).then_inc(w_in[u], 16)
                    sp.dma_start(wu[u][:, :], d.w["eu"][ds(e * P, P), :]).then_inc(w_in[u], 16)
                    sp.dma_start(wd[u][:, :], d.w["ed"][ds(e * P, P), :]).then_inc(w_in[u], 16)

                for u in range(2):
                    load(u, u)
                with sp.Fori(0, HE - 1) as i:
                    for u in range(2):
                        e = i * 2 + u
                        sp.wait_ge(dn_ps, 2 * e + 2)
                        load(e + 2, u)

            @block.gpsimd
            def _(pool):
                by_expert = d.slot_row[:, :].rearrange("p (b e) -> p b e", b=B)

                def gather(i, u):
                    pool.wait_ge(scattered[u], 16 * B * i)
                    pool.tensor_copy(rows[u][:, :].unsqueeze(2), by_expert[:, :, ds(i * 2 + u, 1)]).then_inc(picked, 1)
                    pool.wait_ge(picked, i * 2 + u + 1)
                    pool.wait_ge(t_ps, KC * 2 * i)
                    pool.sem_inc(go, 1)
                    for b in range(B):
                        pool.indirect_dma_start(out=xg[u][:, b * C:(b + 1) * C], out_offset=None, in_=d.xn["n0"],
                                                in_offset=bass.IndirectOffsetOnAxis(ap=rows[u][:, b:b + 1], axis=0)).then_inc(gathered[u], 16)

                def scatter(i, u):
                    pool.wait_ge(eo_done, B * (i * 2 + u + 1))
                    pool.wait_ge(scattered[1 - u], 16 * B * (i + u))
                    pool.sem_inc(go, 1)
                    for b in range(B):
                        pool.indirect_dma_start(out=d.z, out_offset=bass.IndirectOffsetOnAxis(ap=rows[u][:, b:b + 1], axis=0),
                                                in_=eo[u][:, b * C:(b + 1) * C], in_offset=None,
                                                compute_op=ALU.add).then_inc(scattered[u], 16)

                gather(0, 0)
                with pool.Fori(0, HE - 1) as i:
                    gather(i, 1)
                    scatter(i, 0)
                    gather(i + 1, 0)
                    scatter(i, 1)
                gather(HE - 1, 1)
                scatter(HE - 1, 0)
                scatter(HE - 1, 1)
                for u in range(2):
                    pool.wait_ge(scattered[u], 16 * B * HE)

            @block.tensor
            def _(pe):
                def turn(i, u):
                    e = i * 2 + u
                    pe.wait_ge(gathered[u], 16 * B * (i + 1))
                    pe.wait_ge(xt_done, KC * e)
                    for c in range(KC):
                        for b in range(B):
                            last = pe.transpose(ps[c][:, b * P:(b + 1) * P], xg[u][:, b * C + c * P:b * C + (c + 1) * P], ident[:, :])
                        last.then_inc(t_ps, 1)

                def expert(i, u, follow):
                    e = i * 2 + u
                    pe.wait_ge(xt_done, KC * (e + 1))
                    pe.wait_ge(w_in[u], 48 * (i + 1))
                    for f in range(KF):
                        pe.wait_ge(hid_done, KF * e + max(f - 1, 0))
                        for w, bank in ((wg[u], ps[2 + 2 * (f % 2)]), (wu[u], ps[3 + 2 * (f % 2)])):
                            for k in range(KC):
                                last = pe.matmul(bank, w[:, k * F0 + f * P:k * F0 + (f + 1) * P], xT[u][k][:, :], start=k == 0, stop=k == KC - 1)
                        last.then_inc(ffn_ps, 1)
                    follow()
                    pe.wait_ge(eo_done, B * e)
                    pe.wait_ge(hid_done, KF * (e + 1))
                    for b in range(B):
                        for f in range(KF):
                            last = pe.matmul(ps[6 + b // 2][:, (b % 2) * C:(b % 2 + 1) * C], hid[f][:, b * P:(b + 1) * P],
                                             wd[u][:, f * C:(f + 1) * C], start=f == 0, stop=f == KF - 1)
                        if b % 2:
                            last.then_inc(dn_ps, 1)

                pe.wait_ge(consts, 16)
                turn(0, 0)
                with pe.Fori(0, HE - 1) as i:
                    expert(i, 0, lambda: turn(i, 1))
                    expert(i, 1, lambda: turn(i + 1, 0))
                expert(HE - 1, 0, lambda: turn(HE - 1, 1))
                expert(HE - 1, 1, lambda: None)

            @block.scalar
            def _(act):
                def turned(e, u):
                    for c in range(KC):
                        act.wait_ge(t_ps, KC * e + c + 1)
                        act.activation(xT[u][c][:, :], ps[c], ACT.Copy).then_inc(xt_done, 1)

                def gelus(e):
                    for f in range(KF):
                        act.wait_ge(ffn_ps, KF * e + f + 1)
                        act.activation(gel[f % 2][:, :], ps[2 + 2 * (f % 2)], ACT.Gelu).then_inc(gel_done, 1)

                turned(0, 0)
                with act.Fori(0, HE - 1) as i:
                    for u in range(2):
                        gelus(i * 2 + u)
                        turned(i * 2 + u + 1, 1 - u)
                gelus(E0 - 2)
                turned(E0 - 1, 1)
                gelus(E0 - 1)

            @block.vector
            def _(dve):
                with dve.Fori(0, HE) as i:
                    for u in range(2):
                        e = i * 2 + u
                        for f in range(KF):
                            dve.wait_ge(gel_done, KF * e + f + 1)
                            dve.tensor_tensor(out=hid[f][:, :], in0=gel[f % 2][:, :], in1=ps[3 + 2 * (f % 2)], op=ALU.mult).then_inc(hid_done, 1)
                        dve.wait_ge(scattered[u], 16 * B * i)
                        for b in range(B):
                            if b % 2 == 0:
                                dve.wait_ge(dn_ps, 2 * e + b // 2 + 1)
                            dve.tensor_scalar(eo[u][:, b * C:(b + 1) * C], ps[6 + b // 2][:, (b % 2) * C:(b % 2 + 1) * C],
                                              d.slot_w[:, ds(b * E0 + e, 1)], None, ALU.mult).then_inc(eo_done, 1)


RING = 3
UNITS = 2 * TB
LAG = 4
QW = 2 * P
BF16 = mybir.dt.bfloat16


def pair_plan(now, follow):
    plan, x = [], 0

    def add(*event):
        plan.append(event)

    def turned_operands(count):
        nonlocal x
        for _ in range(count if follow else 0):
            add("X", x)
            x += 1

    if now:
        for n in range(LAG, UNITS + LAG):
            add("T", n - LAG)
            if n < UNITS:
                add("S", n)
            elif follow:
                add("N", n - UNITS)
            if (n - LAG) // 2 >= 4:
                add("U", n - LAG)
            if follow and n - LAG < TB:
                add("A", n - LAG)
            more = 2 if 9 <= n < 12 or 13 <= n < 16 else 0
            turned_operands(more // 2)
            if n % 4 == 0 and n > 4:
                add("V", n // 4 - 2)
            if n % 4 == 2 and n > 6:
                add("W", n // 4 - 2)
            turned_operands(more // 2)
        add("V", 3)
        add("W", 3)
    else:
        for n in range(TB):
            add("A", n)
        turned_operands(12)
        for n in range(LAG):
            add("N", n)
    assert x == (12 if follow else 0)
    out, ring = [], 0 if now else 1
    for kind, n in plan:
        out.append((kind, n, ring))
        ring += kind in "TUXWA"
    return out, ring


def attention(nc, d):
    with ExitStack() as ctx:
        s = Scope(nc, "at", ctx)
        h = s.sb("h", KC * T)
        w = [s.sb(f"w{u}", KC * QKV) for u in range(2)]
        wo = s.sb("wo", PAIRS * C)
        cos, sin = s.sb("cos", TB * 2 * DH), s.sb("sin", TB * 4 * DH)
        ident = s.sb("ident", P)
        ident_b, mask_b = s.sb("ident_b", P, BF16), s.sb("mask_b", P, BF16)
        mask = s.sb("mask", P)
        t1, t2, rot = ([s.sb(f"{n}{j}", 4 * DH) for j in range(2)] for n in ("t1", "t2", "rot"))
        parts = s.sb("parts", TB * 12 * DH)
        qT = [[s.sb(f"qT{u}{e}", T, F32R) for e in range(2)] for u in range(2)]
        kT = [[[s.sb(f"kT{u}{e}{o}", T, F32R) for o in range(2)] for e in range(2)] for u in range(2)]
        v = [s.sb(f"v{u}", TB * 2 * DH) for u in range(2)]
        p = [s.sb(f"p{j}", T) for j in range(LAG)]
        pT = [[s.sb(f"pT{j}{e}", (j + 1) * 2 * QW) for e in range(2)] for j in range(4)]
        nmax, rsum = s.sb("nmax", UNITS), s.sb("rsum", UNITS)
        oT = s.sb("oT", T)
        y, y_stage = s.sb("y", TB * C), s.sb("y_stage", TB * C)
        ps = s.banks()
        ring = [ps[4], ps[5], ps[7]]

        def scores(n):
            at = n % 2 * 2 * CH
            return s.all_banks[:, at:at + (n // 2 + 1) * P]

        consts, bf_done = s.sem("consts"), s.sem("bf_done")
        h_in, y_out = s.sem("h_in"), s.sem("y_out")
        w_in = s.sems("w_in")
        qkv_read, rot_done, hi_done, lo_done = (s.sem(x) for x in ("qkv_read", "rot_done", "hi_done", "lo_done"))
        s_ps, max_done, exp_done, inv_done, norm_done = (s.sem(x) for x in ("s_ps", "max_done", "exp_done", "inv_done", "norm_done"))
        full, read = s.sems("full", RING), s.sems("read", RING)
        o_ps, o_done = s.sem("o_ps"), s.sem("o_done")
        y_staged, y_zero = s.sem("y_staged"), s.sem("y_zero")
        zeros_made, slots_zeroed = s.sem("zeros_made"), s.sem("slots_zeroed")
        ZERO_PARTS = SLOTS * C // (P * TB * C)

        FIRST_PLAN, BOTH, LAST = pair_plan(False, True), pair_plan(True, True), pair_plan(True, False)
        R_FIRST, R_PAIR = FIRST_PLAN[1] // RING, BOTH[1] // RING
        assert BOTH[1] % RING == 0 and FIRST_PLAN[1] % RING == 0

        def run(eng, act_on, end=lambda b: None):
            act_on(FIRST_PLAN[0], -1, -1, 1)
            with eng.Fori(0, B - 1) as b:
                with eng.Fori(0, PAIRS // 2) as i:
                    for u in range(2):
                        act_on(BOTH[0], b * PAIRS + (i * 2 + u), i * 2 + u, u)
                end(b)
            it = (B - 1) * PAIRS
            with eng.Fori(0, PAIRS // 2 - 1) as i:
                for u in range(2):
                    act_on(BOTH[0], i * 2 + (it + u), i * 2 + u, u)
            act_on(BOTH[0], it + PAIRS - 2, PAIRS - 2, 0)
            act_on(LAST[0], it + PAIRS - 1, PAIRS - 1, 1)
            end(B - 1)

        def ring_uses(plan, it):
            return 0 if plan is FIRST_PLAN[0] else it * R_PAIR + R_FIRST

        def used(turns, bank):
            return (turns + RING - 1 - bank) // RING

        def part(t, m, o):
            return parts[:, ((t * 4 + m) * 3 + o) * DH:((t * 4 + m) * 3 + o + 2) * DH]

        def tile_parts(t):
            return parts[:, t * 12 * DH:(t + 1) * 12 * DH].rearrange("p (m o c) -> p m o c", m=4, o=3)

        with nc.Block() as block:
            @block.sync
            def _(sp):
                for dst, src in ((ident, d.ident), (mask, d.mask), (wo, d.w["wo1"]), (cos, d.cos), (sin, d.sin)):
                    sp.dma_start(dst[:, :], src).then_inc(consts, 16)

                def open_sequence(b):
                    for c in range(KC):
                        sp.dma_start(h[:, c * T:(c + 1) * T], d.hT1[c * P:(c + 1) * P, ds(b * T, T)]).then_inc(h_in, 16)
                    sp.wait_ge(h_in, (b + 1) * (16 * KC))
                    for u in range(2):
                        sp.dma_start(w[u][:, :], d.w["qkv"][u * P:(u + 1) * P, :]).then_inc(w_in[u], 16)

                def other_weights(b):
                    with sp.Fori(0, PAIRS // 2 - 1) as i:
                        for u in range(2):
                            sp.wait_ge(qkv_read, (b * PAIRS + (i * 2 + u + 1)) * TB)
                            sp.dma_start(w[u][:, :], d.w["qkv"][ds(i * (2 * P) + (2 + u) * P, P), :]).then_inc(w_in[u], 16)

                def store(b):
                    sp.wait_ge(y_staged, b + 1)
                    sp.dma_start(d.y[ds(b * T, T), :].rearrange("(t p) c -> p t c", p=P), tiles(y_stage[:, :], TB)).then_inc(y_out, 16)

                open_sequence(0)
                sp.wait_ge(zeros_made, 1)
                for j in range(ZERO_PARTS):
                    sp.dma_start(d.xd[j * TB * P:(j + 1) * TB * P, :].rearrange("(p r) c -> p (r c)", p=P), y_stage[:, :]).then_inc(slots_zeroed, 16)
                with sp.Fori(0, B - 1) as b:
                    other_weights(b)
                    sp.wait_ge(qkv_read, (b + 1) * (PAIRS * TB))
                    open_sequence(b + 1)
                    store(b)
                other_weights(B - 1)
                store(B - 1)
                sp.wait_ge(slots_zeroed, 16 * ZERO_PARTS)
                sp.wait_ge(y_out, 16 * B)

            @block.tensor
            def _(pe):
                pe.wait_ge(consts, 16 * 5)
                pe.wait_ge(bf_done, 2)
                pe.sem_inc(full[0], 1)
                pe.sem_inc(read[0], 1)

                def act_on(plan, it, pr, u):
                    r, nx = ring_uses(plan, it), it + 1
                    last_x = max([at for what, _, at in plan if what == "X"], default=0) + 1
                    for kind, n, use in plan:
                        if kind == "A":
                            if n == 0:
                                pe.wait_ge(w_in[1 - u], (it + u) * 8 + 16)
                            bank = use % RING
                            pe.wait_ge(read[bank], r + use // RING)
                            for k in range(KC):
                                last = pe.matmul(ring[bank][:, 0:QKV], h[:, k * T + n * P:k * T + (n + 1) * P],
                                                 w[1 - u][:, k * QKV:(k + 1) * QKV], start=k == 0, stop=k == KC - 1)
                            last.then_inc(full[bank], 1)
                        elif kind == "X":
                            m, half = n % 6, n // 6
                            pe.wait_ge(lo_done, nx * TB + 4 * (half + 1))
                            bank = use % RING
                            pe.wait_ge(read[bank], r + use // RING)
                            for t in range(4):
                                src = part(4 * half + t, m if m < 2 else 2 + (m - 2) // 2, int(m in (3, 5)))
                                last = pe.transpose(ring[bank][:, t * P:(t + 1) * P], src, ident[:, :])
                            last.then_inc(full[bank], 1)
                        elif kind in "SN":
                            e, t = n % 2, n // 2
                            of, x = (it, u) if kind == "S" else (nx, 1 - u)
                            if kind == "N" and n == 0:
                                for bank in range(RING):
                                    pe.wait_ge(read[bank], r + used(last_x, bank))
                            if plan is not FIRST_PLAN[0] or n >= 2:
                                pe.wait_ge(exp_done, of * UNITS + (n - 1))
                            width = (t + 1) * P
                            for at in range(0, width, CH):
                                to = min(at + CH, width)
                                bank = ps[2 * e + at // CH]
                                pe.matmul(bank[:, 0:to - at], qT[x][e][:, t * P:(t + 1) * P], kT[x][e][0][:, at:to], start=True, stop=False)
                                if to == width:
                                    pe.matmul(bank[:, to - at - P:to - at], ident_b[:, :], mask_b[:, :], start=False, stop=False,
                                              skip_group_check=True)
                                last = pe.matmul(bank[:, 0:to - at], qT[x][e][:, t * P:(t + 1) * P], kT[x][e][1][:, at:to], start=False, stop=True)
                            last.then_inc(s_ps, 1)
                        elif kind in "TU":
                            pe.wait_ge(norm_done, it * UNITS + n + 1)
                            bank, k0 = use % RING, 4 * (kind == "U")
                            pe.wait_ge(read[bank], r + use // RING)
                            for k in range(k0, min(k0 + 4, n // 2 + 1)):
                                last = pe.transpose(ring[bank][:, (k - k0) * P:(k - k0 + 1) * P], p[n % LAG][:, k * P:(k + 1) * P], ident[:, :])
                            last.then_inc(full[bank], 1)
                        elif kind == "V":
                            before = max(at for what, of, at in plan if what in "TU" and of <= 4 * n + 3) + 1
                            for bank in range(RING):
                                pe.wait_ge(read[bank], r + used(before, bank))
                            pe.wait_ge(o_done, 4 * it + n)
                            for k in range(2 * (n + 1)):
                                skip = max(0, k * P - n * QW)
                                for e in range(2):
                                    last = pe.matmul(ps[6][e * DH:(e + 1) * DH, skip:QW], v[u][:, (k * 2 + e) * DH:(k * 2 + e + 1) * DH],
                                                     pT[n][e][:, k * QW + skip:(k + 1) * QW], start=k == 0, stop=k == 2 * (n + 1) - 1)
                            last.then_inc(o_ps, 1)
                        elif kind == "W":
                            bank = use % RING
                            pe.wait_ge(o_done, 4 * it + n + 1)
                            pe.wait_ge(read[bank], r + use // RING)
                            for t in range(2):
                                last = pe.matmul(ring[bank][:, t * C:(t + 1) * C], oT[:, (2 * n + t) * P:(2 * n + t + 1) * P],
                                                 wo[:, ds(pr * C, C)] if not isinstance(pr, int) else wo[:, pr * C:(pr + 1) * C],
                                                 start=True, stop=True)
                            last.then_inc(full[bank], 1)

                run(pe, act_on)

            @block.scalar
            def _(act):
                act.wait_ge(consts, 16 * 5)
                act.activation(ident_b[:, :], ident[:, :], ACT.Copy).then_inc(bf_done, 1)
                act.activation(mask_b[:, :], mask[:, :], ACT.Copy).then_inc(bf_done, 1)

                def act_on(plan, it, pr, u):
                    r = ring_uses(plan, it)

                    def high(n):
                        act.wait_ge(rot_done, (it + 1) * TB + n + 1)
                        x4 = rot[n % 2][:, :].rearrange("p (m c) -> p m c", m=4).unsqueeze(2).to_broadcast([P, 4, 2, DH])
                        act.activation(tile_parts(n)[:, :, 0:3:2, :].bitcast(F32R), x4, ACT.Copy).then_inc(hi_done, 1)

                    def exp(of, n):
                        act.wait_ge(max_done, of * UNITS + n + 1)
                        act.activation(p[n % LAG][:, 0:(n // 2 + 1) * P], scores(n), ACT.Exp, bias=nmax[:, n:n + 1],
                                       accum_out=rsum[:, n:n + 1]).then_inc(exp_done, 1)

                    for kind, n, use in plan:
                        if kind in "SN":
                            if n >= 1:
                                exp(it if kind == "S" else it + 1, n - 1)
                            elif plan is not FIRST_PLAN[0]:
                                exp(it, UNITS - 1)
                            if n == TB + LAG and plan is not LAST[0]:
                                high(TB - 1)
                        elif kind in "TU":
                            if plan is LAST[0] and kind == "T" and n == UNITS - LAG:
                                exp(it, UNITS - 1)
                            quarter, q = n // 4, n // 2 % 2
                            bank, k0 = use % RING, 4 * (kind == "U")
                            k1 = min(k0 + 4, n // 2 + 1)
                            act.wait_ge(full[bank], r + use // RING + 1)
                            dst = pT[quarter][n % 2][:, k0 * QW:k1 * QW].rearrange("p (k c) -> p k c", c=QW)[:, :, q * P:(q + 1) * P]
                            act.activation(dst, ring[bank][:, 0:(k1 - k0) * P].rearrange("p (k c) -> p k c", c=P), ACT.Copy).then_inc(read[bank], 1)
                        elif kind == "A":
                            if n >= 1:
                                high(n - 1)
                            if n == TB - 1 and plan is FIRST_PLAN[0]:
                                high(n)
                        elif kind == "X":
                            m, half = n % 6, n // 6
                            bank = use % RING
                            act.wait_ge(full[bank], r + use // RING + 1)
                            dst = qT[1 - u][m] if m < 2 else kT[1 - u][(m - 2) // 2][m % 2]
                            act.activation(dst[:, half * CH:(half + 1) * CH], ring[bank], ACT.Copy).then_inc(read[bank], 1)
                        elif kind == "V":
                            act.wait_ge(o_ps, 4 * it + n + 1)
                            act.activation(oT[:, n * QW:(n + 1) * QW], ps[6][:, 0:QW], ACT.Copy).then_inc(o_done, 1)

                run(act, act_on)

            @block.gpsimd
            def _(pool):
                def act_on(plan, it, pr, u):
                    nx = it + 1

                    def rotate(n):
                        pool.wait_ge(lo_done, nx * TB + max(n - 1, 0))
                        pool.wait_ge(qkv_read, nx * TB + n + 1)
                        pool.tensor_tensor(out=rot[n % 2][:, :], in0=t1[n % 2][:, :], in1=t2[n % 2][:, :], op=ALU.add).then_inc(rot_done, 1)

                    def low(n):
                        pool.wait_ge(hi_done, nx * TB + n + 1)
                        x4 = rot[n % 2][:, :].rearrange("p (m c) -> p m c", m=4)
                        p4 = tile_parts(n)
                        pool.tensor_tensor(out=p4[:, :, 1, :], in0=x4, in1=p4[:, :, 0, :], op=ALU.subtract).then_inc(lo_done, 1)

                    if plan is not LAST[0]:
                        for n in range(TB + 1):
                            if n < TB:
                                rotate(n)
                            if n >= 1:
                                low(n - 1)

                run(pool, act_on)

            @block.vector
            def _(dve):
                dve.wait_ge(consts, 16 * 5)

                dve.memset(y_stage[:, :], 0.0).then_inc(zeros_made, 1)
                dve.memset(y[:, :], 0.0).then_inc(y_zero, 1)

                def end(b):
                    for x in range(RING):
                        if isinstance(b, int):
                            dve.wait_ge(read[x], (B * PAIRS - 1) * R_PAIR + R_FIRST + used(LAST[1], x))
                        else:
                            dve.wait_ge(read[x], (b + 1) * (PAIRS * R_PAIR) + R_FIRST)
                    dve.wait_ge(slots_zeroed, 16 * ZERO_PARTS)
                    dve.wait_ge(y_out, b * 16)
                    dve.tensor_copy(y_stage[:, :], y[:, :]).then_inc(y_staged, 1)
                    dve.wait_ge(y_staged, b + 1)
                    dve.memset(y[:, :], 0.0).then_inc(y_zero, 1)
                    dve.wait_ge(y_zero, b + 2)

                def act_on(plan, it, pr, u):
                    r, nx = ring_uses(plan, it), it + 1
                    alone = plan is FIRST_PLAN[0]

                    def invert(of, n):
                        dve.wait_ge(exp_done, of * UNITS + n + 1)
                        dve.reciprocal(rsum[:, n:n + 1], rsum[:, n:n + 1]).then_inc(inv_done, 1)
                        dve.wait_ge(inv_done, of * UNITS + n + 1)
                        buf = p[n % LAG][:, 0:(n // 2 + 1) * P]
                        dve.tensor_scalar(buf, buf, rsum[:, n:n + 1], None, ALU.mult).then_inc(norm_done, 1)

                    for kind, n, use in plan:
                        if kind in "SN":
                            of = it if kind == "S" else nx
                            dve.wait_ge(s_ps, of * UNITS + n + 1)
                            dve.tensor_reduce(out=nmax[:, n:n + 1], in_=scores(n), axis=AX, op=ALU.max, negate=True).then_inc(max_done, 1)
                            if n >= 2:
                                invert(of, n - 2)
                            elif not alone:
                                invert(it, UNITS - 2 + n)
                            if n == UNITS - 1 and plan is LAST[0]:
                                invert(of, n - 1)
                                invert(of, n)
                        elif kind == "A":
                            if not alone or n >= 2:
                                dve.wait_ge(rot_done, nx * TB + (n - 1))
                            bank = use % RING
                            dve.wait_ge(full[bank], r + use // RING + 1)
                            dve.tensor_copy(v[1 - u][:, n * 2 * DH:(n + 1) * 2 * DH], ring[bank][:, 4 * DH:6 * DH])
                            dve.tensor_tensor(out=t1[n % 2][:, :].rearrange("p (m e c) -> p m e c", m=2, e=2),
                                              in0=ring[bank][:, 0:4 * DH].rearrange("p (m e c) -> p m e c", m=2, e=2),
                                              in1=cos[:, n * 2 * DH:(n + 1) * 2 * DH].rearrange("p (m c) -> p m c", m=2).unsqueeze(2).to_broadcast([P, 2, 2, DH]),
                                              op=ALU.mult)
                            dve.tensor_tensor(out=t2[n % 2][:, :].rearrange("p (m h c) -> p m h c", m=4, h=2),
                                              in0=ring[bank][:, 0:4 * DH].rearrange("p (m h c) -> p m h c", m=4, h=2)[:, :, ::-1, :],
                                              in1=sin[:, n * 4 * DH:(n + 1) * 4 * DH].rearrange("p (m h c) -> p m h c", m=4, h=2),
                                              op=ALU.mult).then_inc(qkv_read, 1)
                            dve.wait_ge(qkv_read, nx * TB + n + 1)
                            dve.nop().then_inc(read[bank], 1)
                        elif kind == "W":
                            bank = use % RING
                            if n == 0:
                                for x in range(RING):
                                    dve.wait_ge(read[x], r)
                            dve.wait_ge(full[bank], r + use // RING + 1)
                            part_y = y[:, n * 2 * C:(n + 1) * 2 * C]
                            dve.tensor_tensor(out=part_y, in0=part_y, in1=ring[bank], op=ALU.add).then_inc(read[bank], 1)

                dve.wait_ge(y_zero, 1)
                run(dve, act_on, end)


def route(nc, d):
    with ExitStack() as ctx:
        s = Scope(nc, "rt", ctx)
        W = NT * E1
        ident, before, ones = s.sb("ident", P), s.sb("before", P), s.sb("ones", P)
        logT = s.sb("logT", N, rows=E1)
        br, bias, rank = s.sb("br", E1), s.sb("bias", E1), s.sb("rank", E1)
        tile_no = s.sb("tile_no", SLOT_TILES)
        xn = s.sb("xn", NT * C)
        sc, bi, w, tmp, slot = (s.sb(n, W) for n in ("sc", "bi", "w", "tmp", "slot"))
        m = [s.sb(f"m{k}", W) for k in range(TOP)]
        both, tot, run_ = s.sb("both", W), s.sb("tot", W), s.sb("run", W)
        line = s.sb("line", W)
        top, sums = s.sb("top", NT), s.sb("sums", NT)
        wk = [s.sb(f"wk{k}", NT) for k in range(TOP)]
        cnt, cnt_i, til, end, off = s.sb("cnt", E1), s.sb("cnt_i", E1, I32), s.sb("til", E1), s.sb("end", E1), s.sb("off", E1)
        eid = [s.sb(f"eid{j}", SLOT_TILES) for j in range(2)]
        slot_f = s.sb("slot_f", TOP * NT)
        ps = s.banks()
        consts, log_in, xn_in = s.sem("consts"), s.sem("log_in"), s.sem("xn_in")
        tok_ps, less_max, expd, masks, counted, steps, slots_done, sent = (s.sem(x) for x in (
            "tok_ps", "less_max", "expd", "masks", "counted", "steps", "slots_done", "sent"))

        def te(ap):
            return ap[:, :].rearrange("p (t e) -> p t e", e=E1)

        def et(ap):
            return ap[:, :].rearrange("p (e t) -> p e t", t=NT)

        def over_t(ap):
            return ap[:, :].unsqueeze(1).to_broadcast([P, NT, E1])

        with nc.Block() as block:
            @block.sync
            def _(sp):
                sp.dma_start(logT[:, :], d.logT["n1"]).then_inc(log_in, 16)
                for dst, src in ((ident, d.ident), (before, d.before), (br, d.w["br"]), (bias, d.w["bias"]), (rank, d.rank), (tile_no, d.tile_no)):
                    sp.dma_start(dst[:, :], src).then_inc(consts, 16)
                sp.dma_start(tiles(xn[:, :], NT), d.xn["n1"].rearrange("(t p) c -> p t c", p=P)).then_inc(xn_in, 16)
                for dst, src in ((d.moe_ident, d.ident), (d.moe_w1, d.w["w1"]), (d.moe_w2, d.w["w2"]), (d.moe_b1, d.w["bl1"]), (d.moe_b2, d.w["bl2"])):
                    sp.dma_start(dst[:, :], src).then_inc(d.moe_in, 16)

            @block.gpsimd
            def _(pool):
                pool.wait_ge(xn_in, 16)
                pool.wait_ge(slots_done, 1)
                for k in range(TOP):
                    for t in range(NT):
                        pool.indirect_dma_start(out=d.xd, out_offset=bass.IndirectOffsetOnAxis(ap=d.tok_slot[:, k * NT + t:k * NT + t + 1], axis=0),
                                                in_=xn[:, t * C:(t + 1) * C], in_offset=None).then_inc(sent, 16)
                pool.wait_ge(sent, 16 * TOP * NT)

            @block.tensor
            def _(pe):
                pe.wait_ge(log_in, 16)
                pe.wait_ge(consts, 16 * 6)
                for t in range(NT):
                    last = pe.transpose(ps[0][:, t * E1:(t + 1) * E1], logT[:, t * P:(t + 1) * P], ident[0:E1, 0:E1])
                last.then_inc(tok_ps, 1)
                pe.wait_ge(masks, 1)
                pe.matmul(ps[1][:, 0:W], before[:, :], both[:, :], start=True, stop=True)
                pe.matmul(ps[2][:, 0:W], ones[:, :], both[:, :], start=True, stop=True).then_inc(counted, 1)

            @block.scalar
            def _(act):
                act.wait_ge(less_max, 1)
                act.activation(w[:, :], w[:, :], ACT.Exp).then_inc(expd, 1)

            @block.vector
            def _(dve):
                st = Steps(dve, steps)

                def do(ins):
                    st.done(ins)
                    st.wait()

                dve.wait_ge(tok_ps, 1)
                dve.wait_ge(consts, 16 * 6)
                do(dve.memset(ones[:, :], 1.0))
                do(dve.tensor_tensor(out=te(sc), in0=ps[0][:, 0:W].rearrange("p (t e) -> p t e", e=E1), in1=over_t(br), op=ALU.add))
                st.done(dve.tensor_tensor(out=te(bi), in0=te(sc), in1=over_t(bias), op=ALU.add))
                do(dve.tensor_reduce(out=top[:, :], in_=te(sc), axis=AX, op=ALU.max))
                dve.tensor_tensor(out=te(w), in0=te(sc), in1=bcast(top[:, :], E1), op=ALU.subtract).then_inc(less_max, 1)
                for k in range(TOP):
                    do(dve.tensor_reduce(out=sums[:, :], in_=te(bi), axis=AX, op=ALU.max))
                    do(dve.tensor_tensor(out=te(tmp), in0=te(bi), in1=bcast(sums[:, :], E1), op=ALU.is_equal))
                    do(dve.tensor_tensor(out=te(tmp), in0=te(tmp), in1=over_t(rank), op=ALU.mult))
                    do(dve.tensor_reduce(out=sums[:, :], in_=te(tmp), axis=AX, op=ALU.max))
                    do(dve.tensor_tensor(out=te(m[k]), in0=over_t(rank), in1=bcast(sums[:, :], E1), op=ALU.is_equal))
                    if k == 0:
                        do(dve.scalar_tensor_tensor(out=bi[:, :], in0=m[0][:, :], scalar=-3.0e38, in1=bi[:, :], op0=ALU.mult, op1=ALU.add))
                dve.tensor_tensor(out=both[:, :], in0=m[0][:, :], in1=m[1][:, :], op=ALU.add).then_inc(masks, 1)
                dve.wait_ge(expd, 1)
                do(dve.tensor_reduce(out=sums[:, :], in_=te(w), axis=AX, op=ALU.add))
                do(dve.reciprocal(sums[:, :], sums[:, :]))
                do(dve.tensor_tensor(out=te(w), in0=te(w), in1=bcast(sums[:, :], E1), op=ALU.mult))
                for k in range(TOP):
                    do(dve.tensor_tensor(out=tmp[:, :], in0=w[:, :], in1=m[k][:, :], op=ALU.mult))
                    do(dve.tensor_reduce(out=wk[k][:, :], in_=te(tmp), axis=AX, op=ALU.add))
                do(dve.tensor_tensor(out=sums[:, :], in0=wk[0][:, :], in1=wk[1][:, :], op=ALU.add))
                do(dve.reciprocal(sums[:, :], sums[:, :]))
                for k in range(TOP):
                    st.done(dve.tensor_tensor(out=d.tok_w[:, k * NT:(k + 1) * NT], in0=wk[k][:, :], in1=sums[:, :], op=ALU.mult))
                dve.wait_ge(counted, 1)
                do(dve.tensor_copy(et(tot), ps[2][:, 0:W].rearrange("p (t e) -> p e t", e=E1)))
                do(dve.memset(line[:, :], 1.0))
                do(dve.tensor_tensor_scan(out=run_[:, :], data0=line[:, :], data1=tot[:, :], initial=0.0, op0=ALU.mult, op1=ALU.add))
                do(dve.tensor_reduce(out=cnt[:, :], in_=et(tot), axis=AX, op=ALU.add))
                do(dve.tensor_scalar(til[:, :], cnt[:, :], P - 1.0, None, ALU.add))
                do(dve.tensor_copy(cnt_i[:, :], til[:, :]))
                do(dve.tensor_scalar(cnt_i[:, :], cnt_i[:, :], P.bit_length() - 1, None, ALU.arith_shift_right))
                do(dve.tensor_copy(til[:, :], cnt_i[:, :]))
                do(dve.tensor_tensor_scan(out=end[:, :], data0=line[:, 0:E1], data1=til[:, :], initial=0.0, op0=ALU.mult, op1=ALU.add))
                do(dve.tensor_tensor(out=off[:, :], in0=end[:, :], in1=til[:, :], op=ALU.subtract))
                do(dve.scalar_tensor_tensor(out=off[:, :], in0=off[:, :], scalar=float(P), in1=cnt[:, :], op0=ALU.mult, op1=ALU.add))
                do(dve.tensor_tensor(out=off[:, :], in0=off[:, :], in1=et(run_)[:, :, NT - 1], op=ALU.subtract))
                do(dve.tensor_tensor(out=run_[:, :], in0=run_[:, :], in1=tot[:, :], op=ALU.subtract))
                do(dve.tensor_tensor(out=te(slot), in0=ps[1][:, 0:W].rearrange("p (t e) -> p t e", e=E1),
                                     in1=run_[:, :].rearrange("p (e t) -> p t e", t=NT), op=ALU.add))
                do(dve.tensor_tensor(out=te(slot), in0=te(slot), in1=over_t(off), op=ALU.add))
                for k in range(TOP):
                    do(dve.tensor_tensor(out=tmp[:, :], in0=slot[:, :], in1=m[k][:, :], op=ALU.mult))
                    do(dve.tensor_reduce(out=slot_f[:, k * NT:(k + 1) * NT], in_=te(tmp), axis=AX, op=ALU.add))
                do(dve.tensor_copy(d.tok_slot[:, :], slot_f[:, :]))
                dve.wait_ge(steps, st.k)
                dve.nop().then_inc(slots_done, 1)
                do(dve.memset(eid[0][:, :], 0.0))
                for e in range(E1 - 1):
                    do(dve.scalar_tensor_tensor(out=eid[(e + 1) % 2][:, :], in0=tile_no[:, :], scalar=end[:, e:e + 1], in1=eid[e % 2][:, :],
                                                op0=ALU.is_ge, op1=ALU.add))
                do(dve.tensor_copy(d.tile_expert[:, :], eid[(E1 - 1) % 2][:, :]))


def moe(nc, d):
    with ExitStack() as ctx:
        s = Scope(nc, "moe", ctx)
        w1, w2, b1, b2, ident, consts = d.moe_w1, d.moe_w2, d.moe_b1, d.moe_b2, d.moe_ident, d.moe_in
        xs = [s.sb(f"xs{u}", C) for u in range(2)]
        xT = [s.sb(f"xT{u}", C) for u in range(2)]
        gate, up, hid = ([s.sb(f"{n}{u}", H1) for u in range(2)] for n in ("gate", "up", "hid"))
        hT = s.sb("hT", H1)
        yo = [s.sb(f"yo{u}", C) for u in range(2)]
        ps = s.banks()
        x_in, y_out = s.sems("x_in"), s.sems("y_out")
        xt_ps, xt_done, a_ps, b_ps, a_read, silu_done, b_read, hid_done, ht_ps, ht_done, y_ps, y_done = (s.sem(x) for x in (
            "xt_ps", "xt_done", "a_ps", "b_ps", "a_read", "silu_done", "b_read", "hid_done", "ht_ps", "ht_done", "y_ps", "y_done"))
        L = SLOT_TILES
        IN_LOOP = (L - 2) // 2
        assert L % 2 == 0

        def run(eng, step):
            step(0, 0, True, False)
            with eng.Fori(0, IN_LOOP) as i:
                for u in range(2):
                    step(i * 2 + 1 + u, 1 - u, False, False)
            step(L - 1, 1, False, True)

        def expert_of(eng, j):
            return eng.value_load(d.tile_expert[0:1, ds(j, 1)], min_val=0, max_val=E1 - 1)

        with nc.Block() as block:
            @block.sync
            def _(sp):
                def load(j, u):
                    sp.dma_start(xs[u][:, :], d.xd[ds(j * P, P), :]).then_inc(x_in[u], 16)

                def store(j, u):
                    sp.wait_ge(y_done, j + 1)
                    sp.dma_start(d.yd[ds(j * P, P), :], yo[u][:, :]).then_inc(y_out[u], 16)

                load(0, 0)
                load(1, 1)
                with sp.Fori(0, IN_LOOP) as i:
                    for u in range(2):
                        sp.wait_ge(xt_ps, i * 2 + u + 1)
                        load(i * 2 + u + 2, u)
                        store(i * 2 + u, u)
                store(L - 2, 0)
                store(L - 1, 1)
                for u in range(2):
                    sp.wait_ge(y_out[u], 16 * (L // 2))

            @block.tensor
            def _(pe):
                pe.wait_ge(consts, 16 * 5)

                def turn(j, u, n):
                    pe.wait_ge(x_in[u], n)
                    pe.wait_ge(xt_done, j)
                    for c in range(KC):
                        last = pe.transpose(ps[5][:, c * P:(c + 1) * P], xs[u][:, c * P:(c + 1) * P], ident[:, :])
                    last.then_inc(xt_ps, 1)

                def step(j, u, first, last_one):
                    e = expert_of(pe, j)

                    def half(o, bank, signal):
                        for k in range(KC):
                            last = pe.matmul(bank, xT[u][:, k * P:(k + 1) * P], w1[:, ds(e * (KC * 2 * H1) + (k * 2 + o) * H1, H1)],
                                             start=k == 0, stop=k == KC - 1)
                        last.then_inc(signal, 1)

                    def turn_hidden(j, u):
                        pe.wait_ge(hid_done, j + 1)
                        pe.wait_ge(ht_done, j)
                        for k in range(KH):
                            last = pe.transpose(ps[4][:, k * P:(k + 1) * P], hid[u][:, k * P:(k + 1) * P], ident[:, :])
                        last.then_inc(ht_ps, 1)

                    def down(j):
                        f = expert_of(pe, j)
                        pe.wait_ge(ht_done, j + 1)
                        pe.wait_ge(y_done, j)
                        for k in range(KH):
                            last = pe.matmul(ps[6][:, 0:C], hT[:, k * P:(k + 1) * P], w2[:, ds(f * (KH * C) + k * C, C)], start=k == 0, stop=k == KH - 1)
                        last.then_inc(y_ps, 1)

                    pe.wait_ge(xt_done, j + 1)
                    if not first:
                        pe.wait_ge(a_read, j - 1)
                        pe.wait_ge(b_read, j - 1)
                    half(0, ps[2 * u], a_ps)
                    if not first:
                        turn_hidden(j - 1, 1 - u)
                    half(1, ps[2 * u + 1], b_ps)
                    if not last_one:
                        turn(j + 1, 1 - u, (j + 1 - (1 - u)) * 8 + 16)
                    if not first:
                        down(j - 1)
                    if last_one:
                        turn_hidden(j, u)
                        down(j)

                turn(0, 0, 16)
                run(pe, step)

            @block.scalar
            def _(act):
                def x_turned(j, u):
                    act.wait_ge(xt_ps, j + 1)
                    act.activation(xT[u][:, :], ps[5][:, 0:C], ACT.Copy).then_inc(xt_done, 1)

                def h_turned(j):
                    act.wait_ge(ht_ps, j + 1)
                    act.activation(hT[:, :], ps[4], ACT.Copy).then_inc(ht_done, 1)

                def step(j, u, first, last):
                    if not first:
                        h_turned(j - 1)
                    act.wait_ge(a_read, j + 1)
                    act.activation(gate[u][:, :], gate[u][:, :], ACT.Silu).then_inc(silu_done, 1)
                    if not last:
                        x_turned(j + 1, 1 - u)
                    else:
                        h_turned(j)

                x_turned(0, 0)
                run(act, step)

            @block.vector
            def _(dve):
                dve.wait_ge(consts, 16 * 5)

                def out(j, u, n):
                    e = expert_of(dve, j)
                    dve.wait_ge(y_out[u], n)
                    dve.wait_ge(y_ps, j + 1)
                    dve.tensor_tensor(out=yo[u][:, :], in0=ps[6][:, 0:C], in1=b2[:, ds(e * C, C)], op=ALU.add).then_inc(y_done, 1)

                def step(j, u, first, last):
                    e = expert_of(dve, j)
                    dve.wait_ge(a_ps, j + 1)
                    dve.tensor_tensor(out=gate[u][:, :], in0=ps[2 * u], in1=b1[:, ds(e * (2 * H1), H1)], op=ALU.add).then_inc(a_read, 1)
                    dve.wait_ge(b_ps, j + 1)
                    dve.tensor_tensor(out=up[u][:, :], in0=ps[2 * u + 1], in1=b1[:, ds(e * (2 * H1) + H1, H1)], op=ALU.add).then_inc(b_read, 1)
                    dve.wait_ge(b_read, j + 1)
                    dve.wait_ge(silu_done, j + 1)
                    dve.tensor_tensor(out=hid[u][:, :], in0=gate[u][:, :], in1=up[u][:, :], op=ALU.mult).then_inc(hid_done, 1)
                    if not first:
                        out(j - 1, 1 - u, (j - 2 + u) * 8)
                    if last:
                        out(j, u, (j - u) * 8)

                run(dve, step)


def combine(nc, d):
    with ExitStack() as ctx:
        s = Scope(nc, "fin", ctx)
        y = [[s.sb(f"y{u}{k}", TC * C) for k in range(TOP)] for u in range(2)]
        x, a, th = ([s.sb(f"{n}{u}", TC * C) for u in range(2)] for n in ("x", "a", "th"))
        gathered, loaded, z_done, th_done, out_done, stored = (s.sems(x) for x in ("gathered", "loaded", "z_done", "th_done", "out_done", "stored"))
        steps = s.sem("steps")
        with nc.Block() as block:
            @block.gpsimd
            def _(pool):
                for g in range(NCH):
                    u = g % 2
                    pool.wait_ge(th_done[u], g // 2)
                    pool.wait_ge(stored[u], 16 * (g // 2))
                    for t in range(TC):
                        for k in range(TOP):
                            at = k * NT + g * TC + t
                            pool.indirect_dma_start(out=y[u][k][:, t * C:(t + 1) * C], out_offset=None, in_=d.yd,
                                                    in_offset=bass.IndirectOffsetOnAxis(ap=d.tok_slot[:, at:at + 1], axis=0)).then_inc(gathered[u], 16)

            @block.sync
            def _(sp):
                with sp.Fori(0, NCH // 2) as i:
                    for u in range(2):
                        sp.wait_ge(stored[u], 16 * i)
                        sp.dma_start(tiles(x[u][:, :]), rows_of(d.x2, i * 2 + u)).then_inc(loaded[u], 16)
                        sp.dma_start(tiles(a[u][:, :]), rows_of(d.y, i * 2 + u)).then_inc(loaded[u], 16)
                    for u in range(2):
                        sp.wait_ge(out_done[u], i + 1)
                        sp.dma_start(rows_of(d.out, i * 2 + u), tiles(x[u][:, :])).then_inc(stored[u], 16)
                for u in range(2):
                    sp.wait_ge(stored[u], 16 * (NCH // 2))

            @block.scalar
            def _(act):
                with act.Fori(0, NCH // 2) as i:
                    for u in range(2):
                        act.wait_ge(z_done[u], (i + 1))
                        act.activation(th[u][:, :], y[u][1][:, :], ACT.Tanh, scale=0.5).then_inc(th_done[u], 1)

            @block.vector
            def _(dve):
                st = Steps(dve, steps)
                with dve.Fori(0, NCH // 2) as i:
                    st.loop(i, 2 * (TC + 2))
                    for u in range(2):
                        dve.wait_ge(gathered[u], 16 * TC * TOP * (i + 1))
                        for t in range(TC):
                            cols = slice(t * C, (t + 1) * C)
                            st.done(dve.tensor_scalar(y[u][0][:, cols], y[u][0][:, cols], d.tok_w[:, ds(i * (2 * TC) + u * TC + t, 1)], None, ALU.mult))
                        st.wait()
                        for t in range(TC):
                            cols = slice(t * C, (t + 1) * C)
                            ins = dve.scalar_tensor_tensor(out=y[u][1][:, cols], in0=y[u][1][:, cols],
                                                           scalar=d.tok_w[:, ds(i * (2 * TC) + u * TC + t + NT, 1)],
                                                           in1=y[u][0][:, cols], op0=ALU.mult, op1=ALU.add)
                        ins.then_inc(z_done[u], 1)
                        dve.wait_ge(loaded[u], 32 * (i + 1))
                        dve.wait_ge(z_done[u], i + 1)
                        st.done(dve.tensor_tensor(out=a[u][:, :], in0=y[u][1][:, :], in1=a[u][:, :], op=ALU.mult))
                        dve.wait_ge(th_done[u], i + 1)
                        st.wait()
                        st.done(dve.scalar_tensor_tensor(out=a[u][:, :], in0=th[u][:, :], scalar=1.0, in1=a[u][:, :], op0=ALU.add, op1=ALU.mult))
                        st.wait()
                        dve.scalar_tensor_tensor(out=x[u][:, :], in0=a[u][:, :], scalar=0.5, in1=x[u][:, :], op0=ALU.mult, op1=ALU.add).then_inc(out_done[u], 1)
                st.end(NCH // 2)


class Arrays:
    pass


def build(nc, d):
    def scratch(name, shape):
        return nc.dram_tensor(name, shape, F32, kind="Internal").ap()

    d.xn = {n: scratch("xn_" + n, [N, C]) for n in ("n0", "n1")}
    d.logT = {"n0": scratch("logT_n0", [E0, N]), "n1": scratch("logT_n1", [E1, N])}
    d.s, d.z, d.x2, d.y = (scratch(n, [N, C]) for n in ("s_rows", "z_rows", "x2_rows", "y_rows"))
    d.hT1 = scratch("hT1_cols", [C, N])
    d.xd, d.yd = scratch("slot_in", [SLOTS, C]), scratch("slot_out", [SLOTS, C])

    with ExitStack() as kept:
        k = Scope(nc, "kept0", kept)
        d.slot_row, d.slot_w = k.sb("slot_row", E0 * B, I32), k.sb("slot_w", E0 * B)
        with ExitStack() as wide:
            w = Scope(nc, "wide", wide)
            d.xnT, d.hT = w.sb("xnT", KC * N), w.sb("hT", KC * N)
            normalize(nc, "n0", d, True)
            first_layer(nc, d)
        experts(nc, d)
    normalize(nc, "n1", d, False)
    attention(nc, d)
    with ExitStack() as kept:
        k = Scope(nc, "kept1", kept)
        d.tok_slot, d.tok_w = k.sb("tok_slot", TOP * NT, I32), k.sb("tok_w", TOP * NT)
        d.tile_expert = k.sb("tile_expert", SLOT_TILES, I32)
        with ExitStack() as weights:
            k = Scope(nc, "moe_in", weights)
            d.moe_w1, d.moe_w2 = k.sb("w1", E1 * KC * 2 * H1), k.sb("w2", E1 * KH * C)
            d.moe_b1, d.moe_b2, d.moe_ident = k.sb("b1", E1 * 2 * H1), k.sb("b2", E1 * C), k.sb("ident", P)
            d.moe_in = k.sem("loaded")
            route(nc, d)
            moe(nc, d)
        combine(nc, d)


def kernel(**inputs):
    from concourse import bacc
    from concourse.bass_utils import run_bass_kernel_spmd

    def cols(a):
        rows, m = a.shape
        return a.reshape(rows // P, P, m).transpose(1, 0, 2).reshape(P, rows // P * m)

    def each(a):
        return np.concatenate([cols(m) for m in a], 1)

    def every(a):
        return np.broadcast_to(a.reshape(1, -1), (P, a.size))

    v = {n: np.asarray(a) for n, a in inputs.items()}
    a0, f0, a1, f1 = ({n[len(p):]: a for n, a in v.items() if n.startswith(p)} for p in ("L0_attn_", "L0_ffn_", "L1_attn_", "L1_ffn_"))
    w = {
        "A": a0["A_init"].T, "B": a0["B_init"], "W0": cols(a0["W0"]), "Wo": cols(a0["Wo"].T), "ls": every(a0["ls_g"]),
        "lr": cols(a0["log_lr"][:, None]), "Wk": cols(a0["Wk"].T), "Wv": cols(a0["Wv"].T), "Wq": cols(a0["Wq"].T), "Wg": cols(a0["Wg"].T),
        "Ws_g": cols(f0["Ws_g"].T), "Ws_u": cols(f0["Ws_u"].T), "Ws_d": cols(f0["Ws_d"].T),
        "eg": np.concatenate([cols(m.T) for m in f0["Wg"]]), "eu": np.concatenate([cols(m.T) for m in f0["Wu"]]),
        "ed": np.concatenate([cols(m.T) for m in f0["Wd"]]),
        "wo1": cols(a1["Wo"]),
        "w1": each(f1["Wl1"]), "w2": each(f1["Wl2"]), "bl1": every(f1["bl1"]), "bl2": every(f1["bl2"]),
        "br": every(f1["br"]), "bias": every(f1["biases_N"]),
    }
    three = (a1["Wq"], a1["Wkv"][:, :INNER], a1["Wkv"][:, INNER:])
    w["qkv"] = np.concatenate([cols(np.concatenate([m[:, p * 2 * DH:(p + 1) * 2 * DH] for m in three], 1)) for p in range(PAIRS)])

    freq = (1.0 / 10000.0 ** (np.arange(0, DH, 2, dtype=np.float32) / DH)).astype(np.float32)
    angle = (np.arange(T, dtype=np.float32)[:, None] * freq[None]).astype(np.float64)

    def rotary(lo, hi, heads):
        head = np.concatenate([lo, hi], 1)
        return each([np.concatenate([head * SCALE] * heads + [head] * heads, 1)[t * P:(t + 1) * P] for t in range(TB)]).astype(np.float32)

    tables = {
        "ident": np.eye(P, dtype=np.float32),
        "pos": every((1.0 / (1.0 + 0.1 * np.log(np.arange(1, T + 1, dtype=np.float64)))).astype(np.float32)),
        "row0": (np.arange(B * E0) // E0 * T).astype(np.float32)[:, None],
        "cos": rotary(np.cos(angle), np.cos(angle), 1), "sin": rotary(-np.sin(angle), np.sin(angle), 2),
        "mask": np.triu(np.full((P, P), -3e38, np.float32), 1),
        "before": np.triu(np.ones((P, P), np.float32), 1),
        "rank": every(np.arange(E1, 0, -1, dtype=np.float32)),
        "tile_no": every(np.arange(SLOT_TILES, dtype=np.float32)),
    }

    nc = bacc.Bacc("TRN2", target_bir_lowering=False, num_devices=1)
    arrays = {}

    def given(name, a):
        arrays["in_" + name] = a = np.ascontiguousarray(a)
        return nc.dram_tensor("in_" + name, list(a.shape), mybir.dt.from_np(a.dtype), kind="ExternalInput").ap()

    d = Arrays()
    d.x = given("x", a0["x"].reshape(N, C))
    d.w = {n: given("w_" + n, a) for n, a in w.items()}
    d.gate_w = {"n0": given("gate_w", cols(f0["gate_w"].T)), "n1": given("Wr", cols(f1["Wr"].T))}
    d.gain = {"n0": given("ln_g", cols(a0["ln_g"][:, None])), "n1": given("gamma", cols(a1["gamma"][:, None]))}
    d.off = {"n0": given("ln_b", cols(a0["ln_b"][:, None])), "n1": given("beta", cols(a1["beta"][:, None]))}
    t = {n: given(n, a) for n, a in tables.items()}
    d.ident, d.pos, d.row0, d.cos, d.sin, d.mask = t["ident"], t["pos"], t["row0"], t["cos"], t["sin"], t["mask"]
    d.before, d.rank, d.tile_no = t["before"], t["rank"], t["tile_no"]
    d.out = nc.dram_tensor("out", [N, C], F32, kind="ExternalOutput").ap()
    build(nc, d)
    r = run_bass_kernel_spmd(nc, [arrays], core_ids=[0])
    return r.results[0]["out"].reshape(B, T, C)
```
